# Optimizing a Trainium2 kernel written in Bass

```python
import numpy as np
import jax
import jax.numpy as jnp

def _softmax(x, axis=-1):
    return jax.nn.softmax(x, axis=axis)

def _gelu(x):
    return jax.nn.gelu(x, approximate=True)

def _silu(x):
    return jax.nn.silu(x)

def _sigmoid(x):
    return jax.nn.sigmoid(x)

def _layernorm(x, axis=-1, eps=1e-05):
    m = jnp.mean(x, axis=axis, keepdims=True)
    v = jnp.var(x, axis=axis, keepdims=True)
    return (x - m) / jnp.sqrt(v + eps)

def _scatter_add(tgt, idx, src, axis=0):
    return tgt.at[idx].add(src)

def _segment_sum(src, seg, n):
    return jax.ops.segment_sum(src, seg, n)
kernel_name = 'mk_adaln_ffn_d1_seqx_r4_18b7fc'

def setup_inputs(seed: int=0):
    np.random.seed(seed)
    _w = jnp.asarray

    def _rec_inputs():
        import jax
        import jax.numpy as jnp
        _rk = jax.random.key(seed)
        x = -0.000125 + 0.9999 * jax.random.normal(jax.random.fold_in(_rk, 1), (64, 64, 1024), jnp.float32)
        _lenS = 64 - jax.random.randint(jax.random.fold_in(_rk, 7), (64,), 0, max(1, 64 // 4) + 1, jnp.int32)
        _lenS2 = 64 - jax.random.randint(jax.random.fold_in(_rk, 8), (64,), 0, max(1, 64 // 4) + 1, jnp.int32)
        cond_128 = 0.0061147 + 1.02565 * jax.random.normal(jax.random.fold_in(_rk, 11), (64, 128), jnp.float32)
        return (x, cond_128)
    x, cond_128 = _rec_inputs()

    def _L0_cond_setup():
        import jax, jax.numpy as jnp
        import numpy as np
        K = 8
        T = 1.0
        D_EMBD = 128
        IN_C = 64
        OUT_C = 64
        BS = 32
        H = 1024
        HID = 128
        key = jax.random.key(seed)
        ks = jax.random.split(key, 10)
        s = lambda fan_in: 1.0 / np.sqrt(fan_in)
        return {'x': jax.random.normal(ks[0], (BS, IN_C, H), dtype=jnp.float32), 'embedding': jax.random.normal(ks[1], (BS, D_EMBD), dtype=jnp.float32), 'W0': jax.random.normal(ks[2], (D_EMBD, HID), dtype=jnp.float32) * s(D_EMBD), 'b0': jnp.zeros((HID,), dtype=jnp.float32), 'W1': jax.random.normal(ks[3], (HID, HID), dtype=jnp.float32) * s(HID), 'b1': jnp.zeros((HID,), dtype=jnp.float32), 'W2': jax.random.normal(ks[4], (HID, K), dtype=jnp.float32) * s(HID), 'b2': jnp.zeros((K,), dtype=jnp.float32), 'weight': jax.random.normal(ks[5], (K, OUT_C, IN_C, 1), dtype=jnp.float32) * s(IN_C), 'bias_k': jax.random.normal(ks[6], (K, OUT_C), dtype=jnp.float32) * 0.1}
    _L0_cond_all = _L0_cond_setup()
    _L0_cond_in = {k: v for k, v in _L0_cond_all.items() if k in ('W0', 'b0', 'W1', 'b1', 'W2', 'b2', 'weight', 'bias_k')}
    del _L0_cond_all

    def _L0_ffn_setup():
        import jax, jax.numpy as jnp
        import numpy as np
        EPS = 1e-05

        def _bitlinear(x, w):
            scale = jnp.mean(jnp.abs(w))
            q = jnp.round(jnp.clip(w / (scale + EPS), -1.0, 1.0))
            deq = q * scale
            return x @ deq.T
        key = jax.random.key(seed)
        k1, k2, k3, k4 = jax.random.split(key, 4)
        B, S, H, I = (4, 512, 1024, 2752)
        return {'hidden_states': jax.random.normal(k1, (B, S, H), dtype=jnp.float32), 'w_gate': jax.random.normal(k2, (I, H), dtype=jnp.float32) * 0.02, 'w_up': jax.random.normal(k3, (I, H), dtype=jnp.float32) * 0.02, 'w_down': jax.random.normal(k4, (H, I), dtype=jnp.float32) * 0.02}
    _L0_ffn_all = _L0_ffn_setup()
    _L0_ffn_in = {k: v for k, v in _L0_ffn_all.items() if k in ('w_gate', 'w_up', 'w_down')}
    del _L0_ffn_all
    return {'x': x, 'cond_128': cond_128, 'L0_cond_W0': _L0_cond_in['W0'], 'L0_cond_b0': _L0_cond_in['b0'], 'L0_cond_W1': _L0_cond_in['W1'], 'L0_cond_b1': _L0_cond_in['b1'], 'L0_cond_W2': _L0_cond_in['W2'], 'L0_cond_b2': _L0_cond_in['b2'], 'L0_cond_weight': _L0_cond_in['weight'], 'L0_cond_bias_k': _L0_cond_in['bias_k'], 'L0_ffn_w_gate': _L0_ffn_in['w_gate'], 'L0_ffn_w_up': _L0_ffn_in['w_up'], 'L0_ffn_w_down': _L0_ffn_in['w_down']}

def reference(x, cond_128, L0_cond_W0, L0_cond_b0, L0_cond_W1, L0_cond_b1, L0_cond_W2, L0_cond_b2, L0_cond_weight, L0_cond_bias_k, L0_ffn_w_gate, L0_ffn_w_up, L0_ffn_w_down):
    import jax
    import jax.numpy as jnp

    def _L0_cond_ref(x, embedding, W0, b0, W1, b1, W2, b2, weight, bias_k):
        import jax, jax.numpy as jnp
        import numpy as np
        K = 8
        T = 1.0
        D_EMBD = 128
        IN_C = 64
        OUT_C = 64
        BS = 32
        H = 1024
        HID = 128
        h = jax.nn.gelu(embedding @ W0 + b0, approximate=False)
        h = jax.nn.gelu(h @ W1 + b1, approximate=False)
        att = jax.nn.softmax((h @ W2 + b2) / T, axis=-1)
        agg_w = jnp.einsum('bk,koi->boi', att, weight[..., 0])
        agg_b = att @ bias_k
        out = jnp.einsum('boi,bih->boh', agg_w, x) + agg_b[:, :, None]
        return out

    def _L0_ffn_ref(hidden_states, w_gate, w_up, w_down):
        import jax, jax.numpy as jnp
        import numpy as np
        EPS = 1e-05

        def _bitlinear(x, w):
            scale = jnp.mean(jnp.abs(w))
            q = jnp.round(jnp.clip(w / (scale + EPS), -1.0, 1.0))
            deq = q * scale
            return x @ deq.T
        gate = _bitlinear(hidden_states, w_gate)
        up = _bitlinear(hidden_states, w_up)
        inter = gate * up
        out = _bitlinear(inter, w_down)
        return out
    x = x + _L0_ffn_ref(_L0_cond_ref(x, cond_128, L0_cond_W0, L0_cond_b0, L0_cond_W1, L0_cond_b1, L0_cond_W2, L0_cond_b2, L0_cond_weight, L0_cond_bias_k), L0_ffn_w_gate, L0_ffn_w_up, L0_ffn_w_down)
    return x

_drawn_inputs = setup_inputs


def setup_inputs(seed=0):
    import zlib

    import numpy as np

    out = dict(_drawn_inputs(seed))
    spreads = {'L0_cond_b0': (0.0, 0.8), 'L0_cond_b1': (0.0, 2.0), 'L0_cond_b2': (0.0, 2.0)}
    factors = {'cond_128': 7.162,
     'L0_cond_W0': 6.831,
     'L0_cond_W1': 6.348,
     'L0_cond_W2': 6.016,
     'L0_cond_weight': 2.848,
     'L0_cond_bias_k': 8.0,
     'L0_ffn_w_gate': 2.936,
     'L0_ffn_w_up': 2.809,
     'L0_ffn_w_down': 2.813}
    for name, (base, spread) in spreads.items():
        noise = np.random.default_rng([zlib.crc32(name.encode()), seed]).standard_normal(out[name].shape)
        drawn = base * np.exp(spread * noise) if base else spread * noise
        out[name] = jnp.asarray(drawn.astype(out[name].dtype))
    for name, factor in factors.items():
        out[name] = (out[name] * factor).astype(out[name].dtype)
    return out
```

```python
import concourse.bass as bass
from concourse import mybir
from contextlib import ExitStack


def adaln_ternary_ffn(nc: bass.Bass, x, cond, w0, b0, w1, b1, w2, b2, wk, bias_k, w_gate, w_up, w_down, out):
    f32, bf16, f16, f8, i32 = (mybir.dt.float32, mybir.dt.bfloat16, mybir.dt.float16,
                               mybir.dt.float8e4, mybir.dt.int32)
    ALU, ACT, AX = mybir.AluOpType, mybir.ActivationFunctionType, mybir.AxisListType

    P = 128
    B, C, H = x.shape
    F = w_gate.shape[0]
    NK = wk.shape[0]
    EPS = 1e-5
    TOK = 512
    NT = TOK // P
    NC = B * C // TOK
    BC = TOK // C
    KH = H // P
    FT = F // P
    FR = F - FT * P
    assert FR == 64 and C == 64
    GU = 2 * FT + 1
    UP = FT + 1
    HB = H // TOK
    DN = NT * HB
    OO = P // NK
    OG = C // OO
    CT = 1024
    DP = -(-F // CT)
    L1_LOG = 14
    PROD = 2.0 ** -15
    EXPONENT = 0x7F800000

    raw = []
    for m, w in enumerate((w_gate, w_up)):
        for use in ("sum", "quant"):
            for f in range(FT + 1):
                rows = P if f < FT else FR
                reader = "act" if (m, use) == (0, "sum") else "dve"
                raw.append((reader, w[f * P:f * P + rows, :], rows, H))
    for use in ("sum", "quant"):
        for r in range(KH):
            for m in range(DP):
                cols = min(CT, F - m * CT)
                raw.append(("act" if use == "sum" else "dve",
                            w_down[r * P:(r + 1) * P, m * CT:m * CT + cols], P, cols))
    NG, ND = FT + 1, KH * DP
    G_SUM, G_Q, U_SUM, U_Q, D_SUM, D_Q = 0, NG, 2 * NG, 3 * NG, 4 * NG, 4 * NG + ND
    NQ = 2 * NG + ND
    RING = 5

    def q_entry(n):
        return G_Q + n if n < NG else U_Q + n - NG if n < 2 * NG else D_Q + n - 2 * NG

    def freed(n):
        who = raw[n][0]
        return who, sum(1 for e in raw[:n + 1] if e[0] == who)

    order0 = [("T", 0), ("T", 1)]
    t_up, t_dn, s_dn = 2, 2 * NG, 0
    for f in range(FT):
        order0.append(("G", f))
        for _ in range(1 if f < 6 else 2):
            if t_up < NG or f >= 13:
                order0.append(("T", t_up))
                t_up += 1
    while t_up < 2 * NG:
        order0.append(("T", t_up))
        t_up += 1
    for u in range(UP):
        order0.append(("U", u))
        if u < 8:
            for _ in range(3):
                order0.append(("S", s_dn))
                s_dn += 1
        if u >= 9 and u - 9 < ND // 2:
            for _ in range(2):
                order0.append(("T", t_dn))
                t_dn += 1
    assert s_dn == ND and t_dn == NQ

    ctx = ExitStack()
    with ctx:
        def sb(name, shape, dt):
            return ctx.enter_context(nc.sbuf_tensor(name, shape, dt))

        def sem(name):
            return ctx.enter_context(nc.semaphore(name))

        wgT = sb("wgT", [P, KH, FT * P], f8)
        wuT = sb("wuT", [P, KH, FT * P], f8)
        wrT = sb("wrT", [P, KH, 2 * FR], f8)
        wdT = sb("wdT", [P, FT + 1, H], f8)
        inter = sb("inter", [P, FT, TOK], f32)
        inter_r = sb("inter_r", [P, TOK], f16)
        yp = sb("yp", [P, KH, 2, TOK], f16)
        ys = sb("ys", [P, KH, TOK], f32)
        xa = sb("xa", [P, NT, H], f32)
        xr = sb("xr", [P, NT, H], f32)
        aT = sb("aT", [P, B // 2, C], f32)
        ablk = sb("ablk", [P, NT, P], f32)
        bprod = sb("bprod", [NK, TOK], f32)
        bbc = sb("bbc", [P, TOK], f32)
        prod = sb("prod", [P, 2, TOK], f32)
        g_r = sb("g_r", [P, TOK], f32)
        hi_r = sb("hi_r", [P, TOK], f16)
        ab = sb("ab", [P, 2, TOK], bf16)
        l1 = sb("l1", [P, TOK], bf16)
        p2 = sb("p2", [P, TOK], f32)
        scl = bbc
        raw5 = sb("raw5", [P, CT], f32)
        msk = sb("msk", [P, 2, CT], bf16)
        identb = sb("identb", [P, P], bf16)
        onesb = sb("onesb", [P, P], bf16)
        ones = sb("ones", [P, P], f32)
        attT = sb("attT", [NK, B], f32)
        biask = sb("biask", [NK, C], f32)
        wsum = sb("wsum", [P, ND], f32)
        tot = sb("tot", [P, 3], f32)
        mean = sb("mean", [P, 3], f32)
        den = sb("den", [P, 3], f32)
        thr = sb("thr", [P, 3], f32)
        nthr = sb("nthr", [P, 3], f32)
        kk = sb("kk", [P, 3], f32)
        p2t = sb("p2t", [P, NT], f32)
        osc = sb("osc", [P, NT], f32)

        ring = [xr[:, t, :] for t in range(NT)] + [raw5[:, :]]
        assert len(ring) == RING and CT == H

        def part(f, i):
            return inter[:, f, :].bitcast(f16)[:, i * TOK:(i + 1) * TOK]

        def early(n):
            return inter[:, n, :]
        w0_sb, w1_sb = early(0)[:, 0:P], early(0)[:, P:2 * P]
        w2_sb = early(0)[:, 2 * P:2 * P + NK]
        b0_sb, b1_sb = early(0)[:, 272:273], early(0)[:, 273:274]
        b2_sb = early(0)[0:B, 280:280 + NK]
        lg = early(0)[0:B, 290:290 + NK]
        ex = early(0)[0:B, 300:300 + NK]
        att = early(0)[0:B, 310:310 + NK]
        nmx, esum, rsum = (early(0)[0:B, 320 + i:321 + i] for i in range(3))
        mask = early(0)[:, 330:330 + OO]
        cond_sb, condT = early(1)[0:B, 0:P], early(1)[:, P:P + B]
        h1, h2 = early(1)[:, 192:192 + B], early(1)[:, 256:256 + B]
        attr = early(1)[0:B, 320:320 + P]
        attrT = early(1)[:, 448:448 + B]
        ident = early(2)[:, 0:P]
        wk_sb = inter[:, 3, :].rearrange("p (g d i) -> p g d i", g=OG, d=2)
        attd = inter[:, 4:6, :].rearrange("p a n -> p (a n)").rearrange("p (o b) -> p o b", b=B)

        ps = [ctx.enter_context(nc.psum_tensor(f"ps{i}", [P, TOK], f32)) for i in range(8)]
        GUB, DNB, YB = ps[0:4], ps[4:6], ps[6:8]
        psb = [p[:, :].bitcast(bf16) for p in ps]

        s_cond = sem("s_cond")
        s_ident0 = sem("s_ident0")
        s_ident = sem("s_ident")
        s_pe = sem("s_pe")
        s_cv = sem("s_cv")
        s_ca = sem("s_ca")
        s_agg = sem("s_agg")
        s_aggv = sem("s_aggv")
        s_raw = [sem(f"s_raw{i}") for i in range(RING)]
        s_raw_free = {"act": sem("s_raw_act"), "dve": sem("s_raw_dve")}
        s_usum = sem("s_usum")
        s_tot = sem("s_tot")
        s_totm = sem("s_totm")
        s_mean, s_den, s_thr = sem("s_mean"), sem("s_den"), sem("s_thr")
        s_gt = sem("s_gt")
        s_q = sem("s_q")
        s_t = sem("s_t")
        s_te = sem("s_te")
        s_x = sem("s_x")
        s_xr = sem("s_xr")
        s_ablk = sem("s_ablk")
        s_bprod = sem("s_bprod")
        s_bb = sem("s_bb")
        s_bbv = sem("s_bbv")
        s_y = sem("s_y")
        s_yv = sem("s_yv")
        s_abs = sem("s_abs")
        s_l1 = sem("s_l1")
        s_norm = sem("s_norm")
        s_pos = sem("s_pos")
        s_p2 = sem("s_p2")
        s_scl = sem("s_scl")
        s_p2T = sem("s_p2T")
        s_p2v = sem("s_p2v")
        s_osc = sem("s_osc")
        s_ysc = sem("s_ysc")
        s_yhi = sem("s_yhi")
        s_ylo = sem("s_ylo")
        s_gu = sem("s_gu")
        s_gv = sem("s_gv")
        s_gr = sem("s_gr")
        s_uv = sem("s_uv")
        s_hir = sem("s_hir")
        s_uhi = sem("s_uhi")
        s_ulo = sem("s_ulo")
        s_dn = sem("s_dn")
        s_o = sem("s_o")
        s_kk = sem("s_kk")
        s_turn_pe, s_turn_pool = sem("s_turn_pe"), sem("s_turn_pool")
        s_st = [sem(f"s_st{t}") for t in range(NT)]

        xt = x.rearrange("(t b) c h -> t (b c) h", b=2)
        ot = out.rearrange("(t b) c h -> t (b c) h", b=2)

        block = ctx.enter_context(nc.Block())

        @block.sync
        def _(sp):
            for dst, src in ((cond_sb, cond), (w0_sb, w0), (b0_sb, b0[:, None]), (w1_sb, w1), (b1_sb, b1[:, None]),
                             (w2_sb, w2), (b2_sb, b2[None, :].broadcast_to([B, NK])),
                             (wk_sb[:, :, 0, :], wk.rearrange("k (a g) i z -> (k a) g (i z)", g=OG)),
                             (wk_sb[:, :, 1, :], wk.rearrange("k (a g) i z -> (k a) g (i z)", g=OG)),
                             (biask[:, :], bias_k)):
                sp.dma_start(dst, src).then_inc(s_cond, 16)

            def load_x(c):
                sp.dma_start(xa[:, :, :], xt[bass.ds(c * NT, NT), :, :].rearrange("t p h -> p t h")).then_inc(s_x, 16)

            def store(c):
                for d in range(DN):
                    t, n = d // HB, d % HB
                    sp.wait_ge(s_o, DN * c + d + 1)
                    sp.dma_start(ot[c * NT + t, :, n * TOK:(n + 1) * TOK],
                                 xr[:, t, n * TOK:(n + 1) * TOK]).then_inc(s_st[t], 16)

            for n, (_, src, rows, cols) in enumerate(raw):
                if n == 6:
                    load_x(0)
                if n >= RING:
                    who, count = freed(n - RING)
                    sp.wait_ge(s_raw_free[who], count)
                sp.dma_start(ring[n % RING][0:rows, 0:cols], src).then_inc(s_raw[n % RING], 16)

            sp.wait_ge(s_xr, NT)
            sp.wait_ge(s_y, KH)
            load_x(1)
            store(0)
            with sp.Fori(1, NC - 1) as c:
                sp.wait_ge(s_xr, NT * c + NT)
                sp.wait_ge(s_y, KH * c + KH)
                load_x(c + 1)
                store(c)
            store(NC - 1)
            for t in range(NT):
                sp.wait_ge(s_st[t], 16 * HB * NC)

        def raw_arrived(eng, n):
            eng.wait_ge(s_raw[n % RING], 16 * (n // RING + 1))

        @block.gpsimd
        def _(pool):
            nc.gpsimd.memset(identb[:, :], 0.0).then_inc(s_ident0, 1)
            nc.gpsimd.memset(ident, 0.0).then_inc(s_ident0, 1)
            nc.gpsimd.memset(ones[:, :], 1.0)
            nc.gpsimd.memset(onesb[:, :], 1.0)
            nc.gpsimd.memset(wsum[:, :], 0.0)
            nc.gpsimd.memset(ablk[:, :, :], 0.0)
            pool.wait_ge(s_ident0, 2)
            for m in (ident, identb[:, :]):
                nc.gpsimd.affine_select(out=m, in_=m, compare_op=ALU.not_equal, fill=1.0, base=0,
                                        pattern=[[-1, P]], channel_multiplier=1).then_inc(s_ident, 1)
            def next_chunk(c):
                pool.wait_ge(s_aggv, 4 * OG)
                pool.sem_inc(s_turn_pool, 1)
                for h in range(2):
                    if h == 1:
                        pool.wait_ge(s_ablk, 2 * c + 1)
                        pool.sem_inc(s_turn_pool, 1)
                    nc.gpsimd.tensor_copy(ablk[h * C:(h + 1) * C, :, h * C:(h + 1) * C],
                                          aT[h * C:(h + 1) * C, bass.ds(c * NT, NT), :]).then_inc(s_ablk, 1)
                pool.wait_ge(s_ablk, 2 * c + 2)
                nc.gpsimd.tensor_tensor(
                    bprod[:, :].rearrange("k (b o) -> k b o", o=C),
                    attT[:, bass.ds(c * BC, BC)].unsqueeze(2).broadcast_to([NK, BC, C]),
                    biask[:, :].unsqueeze(1).broadcast_to([NK, BC, C]), ALU.mult).then_inc(s_bprod, 1)

            def residual(c):
                pool.wait_ge(s_x, 16 * (c + 1))
                pool.wait_ge(s_raw_free["dve"], freed(len(raw) - 1)[1])
                pool.sem_inc(s_turn_pool, 1)
                for t in range(NT):
                    nc.gpsimd.tensor_copy(xr[:, t, :], xa[:, t, :]).then_inc(s_xr, 1)

            next_chunk(0)
            pool.wait_ge(s_bprod, 1)
            for n in range(NQ):
                m, e = min(n // NG, 2), q_entry(n)
                rows, cols = raw[e][2:]
                raw_arrived(pool, e)
                if n in (0, NG, 2 * NG):
                    pool.wait_ge(s_thr, m + 1)
                if n >= 2:
                    pool.wait_ge(s_t, n - 1)
                nc.gpsimd.tensor_scalar(msk[0:rows, n % 2, 0:cols], ring[e % RING][0:rows, 0:cols],
                                        thr[0:rows, m:m + 1], None, ALU.is_gt).then_inc(s_gt, 1)
            residual(0)

            def chunk(c):
                pool.wait_ge(s_y, KH * c + KH)
                pool.wait_ge(s_bb, c + 1)
                pool.wait_ge(s_xr, NT * c + NT)
                next_chunk(c + 1)
                pool.wait_ge(s_bprod, c + 2)
                for t in range(NT):
                    pool.wait_ge(s_st[t], 16 * HB * (c + 1))
                residual(c + 1)

            chunk(0)
            with pool.Fori(1, NC - 1) as c:
                chunk(c)

        @block.tensor
        def _(pe):
            def mm(o, l, r, start=True, stop=True):
                return nc.tensor.matmul(o, l, r, start=start, stop=stop)

            pe.wait_ge(s_ident, 2)
            pe.wait_ge(s_cond, 160)
            nc.tensor.transpose(ps[0][:, 0:B], cond_sb, ident[0:B, 0:B]).then_inc(s_pe, 1)
            pe.wait_ge(s_cv, 1)
            mm(ps[1][:, 0:B], w0_sb, condT).then_inc(s_pe, 1)
            pe.wait_ge(s_ca, 1)
            mm(ps[2][:, 0:B], w1_sb, h1).then_inc(s_pe, 1)
            pe.wait_ge(s_ca, 2)
            mm(ps[3][0:B, 0:NK], h2, w2_sb).then_inc(s_pe, 1)
            pe.wait_ge(s_cv, 6)
            nc.tensor.transpose(ps[4][0:NK, 0:B], att, ident[0:B, 0:B]).then_inc(s_pe, 1)
            pe.wait_ge(s_cv, 7)
            nc.tensor.transpose(ps[5][:, 0:B], attr, ident[0:B, 0:B]).then_inc(s_pe, 1)
            pe.wait_ge(s_cv, 11)
            for g in range(OG):
                for h in range(2):
                    mm(ps[2 * g + h][:, :], wk_sb[:, g, :, :].rearrange("p d i -> p (d i)"),
                       attd[:, h * (OO // 2):(h + 1) * (OO // 2), :].rearrange("p o b -> p (o b)")).then_inc(s_agg, 1)

            def agg_b(c):
                pe.wait_ge(s_bprod, c + 1)
                if isinstance(c, int) and c == 0:
                    pe.wait_ge(s_aggv, 4 * OG)
                else:
                    pe.wait_ge(s_osc, c)
                mm(YB[1][:, :], ones[0:NK, :], bprod[:, :]).then_inc(s_bb, 1)

            def conv(c, k):
                if k == 0:
                    pe.wait_ge(s_x, 16 * (c + 1))
                    pe.wait_ge(s_ablk, 2 * (c + 1))
                if k == 1:
                    pe.wait_ge(s_bbv, c + 1)
                if k >= 2:
                    pe.wait_ge(s_yv, KH * c + k - 1)
                for t in range(NT):
                    last = mm(YB[k % 2][:, t * P:(t + 1) * P], xa[:, t, k * P:(k + 1) * P], ablk[:, t, :])
                last.then_inc(s_y, 1)

            def norms(c):
                pe.wait_ge(s_l1, KH * (c + 1))
                mm(YB[0][:, :], onesb[:, :], l1[:, :]).then_inc(s_norm, 1)

            def norms_T(c):
                pe.wait_ge(s_p2, c + 1)
                for t in range(NT):
                    last = mm(YB[1][:, t:t + 1], p2[0:1, t * P:(t + 1) * P], ones[0:1, 0:1])
                last.then_inc(s_p2T, 1)

            def total(m):
                pe.wait_ge(s_tot, m + 1)
                if m == 0:
                    pe.wait_ge(s_pos, 1)
                else:
                    pe.wait_ge(s_mean, m)
                mm(YB[0][:, 0:1], ones[:, :], tot[:, m:m + 1]).then_inc(s_totm, 1)

            def transpose(n):
                rows, cols = raw[q_entry(n)][2:]
                pe.wait_ge(s_q, n + 1)
                if n >= 2:
                    pe.wait_ge(s_te, n - 1)
                bank = psb[4 + n % 2]
                nb = -(-cols // P)
                for q in range(nb):
                    w = min(P, cols - q * P)
                    last = nc.tensor.transpose(bank[0:w, q * P:q * P + rows], msk[0:rows, n % 2, q * P:q * P + w],
                                               identb[0:rows, 0:rows])
                last.then_inc(s_t, 1)

            def waited(c):
                if not isinstance(c, int):
                    pe.sem_inc(s_turn_pe, 1)

            def group(c, j):
                if j == 0:
                    pe.wait_ge(s_ylo, KH * (c + 1))
                if j < 4:
                    if not (isinstance(c, int) and c == 0):
                        pe.wait_ge(s_uv, UP * c)
                elif j - 4 < FT:
                    pe.wait_ge(s_gv, FT * c + j - 3)
                else:
                    pe.wait_ge(s_uv, UP * c + j - 3 - FT)
                waited(c)
                for k in range(KH):
                    if j < FT:
                        w = wgT[:, k, j * P:(j + 1) * P]
                    elif j == FT:
                        w = wrT[:, k, :]
                    else:
                        w = wuT[:, k, (j - UP) * P:(j - UP + 1) * P]
                    for i in range(2):
                        last = mm(GUB[j % 4][:, :], w, yp[:, k, i, :], start=(k + i == 0), stop=(k == KH - 1 and i == 1))
                last.then_inc(s_gu, 1)

            def down(c, d):
                t, n = d // HB, d % HB
                if d >= 2:
                    pe.wait_ge(s_o, DN * c + d - 1)
                elif isinstance(c, int) and c == 0:
                    pe.wait_ge(s_te, NQ)
                else:
                    pe.wait_ge(s_o, DN * c)
                cols = slice(n * TOK, (n + 1) * TOK)
                if d == 0:
                    pe.wait_ge(s_ulo, UP * c + 1)
                waited(c)
                mm(DNB[d % 2][:, :], inter_r[:, t * P:(t + 1) * P], wdT[:, FT, cols], start=True, stop=False)
                for f in range(FT):
                    if d == 0:
                        pe.wait_ge(s_ulo, UP * c + f + 2)
                        waited(c)
                    for i in range(2):
                        last = mm(DNB[d % 2][:, :], part(f, i)[:, t * P:(t + 1) * P], wdT[:, f, cols],
                                  start=False, stop=(f == FT - 1 and i == 1))
                last.then_inc(s_dn, 1)

            def downs(c, more):
                for d in range(DN):
                    down(c, d)
                    if more and d == 0:
                        norms(c + 1)
                    if more and d == 1:
                        norms_T(c + 1)

            agg_b(0)
            for k in range(KH):
                conv(0, k)
            norms(0)
            norms_T(0)
            total(0)
            for what, n in order0:
                if what == "T":
                    if n == NG:
                        total(1)
                    if n == 2 * NG:
                        total(2)
                    transpose(n)
                elif what == "G":
                    if n == 0:
                        pe.wait_ge(s_te, 1)
                    else:
                        pe.wait_ge(s_te, n + 1)
                    group(0, n)
                elif what == "U":
                    pe.wait_ge(s_te, 2 * NG if n == 0 else NG + n)
                    group(0, FT + n)
            agg_b(1)
            for k in range(KH):
                conv(1, k)
            downs(0, True)

            def chunk(c, more):
                for j in range(GU):
                    group(c, j)
                    if more and j == UP + 9:
                        agg_b(c + 1)
                    if more and j - UP - 11 in range(KH):
                        conv(c + 1, j - UP - 11)
                downs(c, more)

            with pe.Fori(1, NC - 1) as c:
                chunk(c, True)
            chunk(NC - 1, False)

        @block.scalar
        def _(act):
            act.wait_ge(s_pe, 2)
            nc.scalar.activation(h1, ps[1][:, 0:B], ACT.Gelu, bias=b0_sb).then_inc(s_ca, 1)
            act.wait_ge(s_pe, 3)
            nc.scalar.activation(h2, ps[2][:, 0:B], ACT.Gelu, bias=b1_sb).then_inc(s_ca, 1)
            act.wait_ge(s_cv, 3)
            nc.scalar.activation(ex, lg, ACT.Exp, bias=nmx, accum_out=esum).then_inc(s_ca, 1)

            def raw_sum(e, col):
                rows, cols = raw[e][2:]
                raw_arrived(act, e)
                nc.scalar.activation(ring[e % RING][0:rows, 0:cols], ring[e % RING][0:rows, 0:cols], ACT.Abs,
                                     accum_out=wsum[0:rows, col:col + 1]).then_inc(s_raw_free["act"], 1)

            def copy_T(n):
                act.wait_ge(s_t, n + 1)
                bank = psb[4 + n % 2]
                if n < 2 * NG:
                    f = n % NG
                    if f < FT:
                        dst = (wgT, wuT)[n // NG][:, :, f * P:(f + 1) * P]
                        src = bank[:, 0:KH * P].rearrange("p (k f) -> p k f", f=P)
                    else:
                        dst = wrT[:, :, (n // NG) * FR:(n // NG + 1) * FR]
                        src = bank[:, 0:KH * P].rearrange("p (k f) -> p k f", f=P)[:, :, 0:FR]
                    nc.scalar.copy(dst, src, saturate=False).then_inc(s_te, 1)
                    return
                r, m = divmod(n - 2 * NG, DP)
                f0, nf = m * (CT // P), min(CT // P, FT - m * (CT // P))
                last = nc.scalar.copy(wdT[:, f0:f0 + nf, r * P:(r + 1) * P],
                                      bank[:, 0:nf * P].rearrange("p (f h) -> p f h", h=P), saturate=False)
                if f0 + nf == FT:
                    for h in range(2):
                        last = nc.scalar.copy(wdT[h * FR:(h + 1) * FR, FT, r * P:(r + 1) * P],
                                              bank[0:FR, nf * P:(nf + 1) * P], saturate=False)
                last.then_inc(s_te, 1)

            def magnitudes(c, k):
                act.wait_ge(s_yv, KH * c + k + 1)
                if k >= 2:
                    act.wait_ge(s_l1, KH * c + k - 1)
                elif not (isinstance(c, int) and c == 0):
                    act.wait_ge(s_l1, KH * c)
                nc.scalar.activation(ab[:, k % 2, :], ys[:, k, :], ACT.Abs).then_inc(s_abs, 1)

            def split_y(c):
                for k in range(KH):
                    act.wait_ge(s_ysc, KH * c + k + 1)
                    nc.scalar.copy(yp[:, k, 0, :], ys[:, k, :]).then_inc(s_yhi, 1)

            def gate(c, f):
                act.wait_ge(s_gu, GU * c + f + 1)
                if f == 0 and not (isinstance(c, int) and c == 0):
                    act.wait_ge(s_dn, DN * c)
                nc.scalar.copy(inter[:, f, :], GUB[f % 4][:, :]).then_inc(s_gv, 1)

            def up(c, u):
                if u == 0:
                    act.wait_ge(s_gu, GU * c + FT + 1)
                    nc.scalar.copy(g_r[C:P, :], GUB[FT % 4][0:C, :]).then_inc(s_gr, 1)
                    act.wait_ge(s_uv, UP * c + 1)
                    nc.scalar.copy(hi_r[C:P, :], prod[C:P, 0, :]).then_inc(s_hir, 1)
                    nc.scalar.copy(inter_r[0:C, :], prod[C:P, 0, :]).then_inc(s_uhi, 1)
                else:
                    act.wait_ge(s_uv, UP * c + u + 1)
                    nc.scalar.copy(part(u - 1, 0), prod[:, u % 2, :]).then_inc(s_uhi, 1)

            for n in range(NG // 2):
                raw_sum(G_SUM + n, n)
            for k in range(KH):
                magnitudes(0, k)
            for n in range(NG // 2, NG):
                raw_sum(G_SUM + n, n)
            split_y(0)
            for what, n in order0:
                if what == "T":
                    copy_T(n)
                elif what == "G":
                    gate(0, n)
                elif what == "U":
                    up(0, n)
                else:
                    if n == 0:
                        act.wait_ge(s_tot, 2)
                    raw_sum(D_SUM + n, n)
            for k in range(KH):
                magnitudes(1, k)
            split_y(1)

            def chunk(c, more):
                for f in range(FT):
                    gate(c, f)
                for u in range(UP):
                    up(c, u)
                    if more and u - 12 in range(KH):
                        magnitudes(c + 1, u - 12)
                if more:
                    split_y(c + 1)

            with act.Fori(1, NC - 1) as c:
                chunk(c, True)
            chunk(NC - 1, False)

        @block.vector
        def _(dve):
            V = nc.vector
            dve.wait_ge(s_pe, 1)
            V.tensor_copy(condT, ps[0][:, 0:B]).then_inc(s_cv, 1)
            dve.wait_ge(s_pe, 4)
            V.tensor_tensor(lg, ps[3][0:B, 0:NK], b2_sb, ALU.add).then_inc(s_cv, 1)
            dve.wait_ge(s_cv, 2)
            V.tensor_reduce(nmx, lg, AX.X, ALU.max, negate=True).then_inc(s_cv, 1)
            dve.wait_ge(s_ca, 3)
            V.reciprocal(rsum, esum).then_inc(s_cv, 1)
            dve.wait_ge(s_cv, 4)
            V.tensor_scalar(att, ex, rsum, None, ALU.mult).then_inc(s_cv, 1)
            V.tensor_reduce(mask, ident.rearrange("p (k o) -> p o k", o=OO), AX.X, ALU.add).then_inc(s_cv, 1)
            dve.wait_ge(s_cv, 5)
            V.tensor_copy(attr.rearrange("b (k o) -> b k o", o=OO),
                          att.unsqueeze(2).broadcast_to([B, NK, OO])).then_inc(s_cv, 1)
            dve.wait_ge(s_pe, 5)
            V.tensor_copy(attT[:, :], ps[4][0:NK, 0:B]).then_inc(s_cv, 1)
            dve.wait_ge(s_pe, 6)
            V.tensor_copy(attrT, ps[5][:, 0:B]).then_inc(s_cv, 1)
            dve.wait_ge(s_cv, 9)
            half = OO // 2
            for h in range(2):
                V.tensor_tensor(attd[:, h * half:(h + 1) * half, :], attrT.unsqueeze(1).broadcast_to([P, half, B]),
                                mask[:, h * half:(h + 1) * half].unsqueeze(2).broadcast_to([P, half, B]),
                                ALU.mult).then_inc(s_cv, 1)
            for g in range(OG):
                for h in range(2):
                    dve.wait_ge(s_agg, 2 * g + h + 1)
                    src = ps[2 * g + h][:, :].rearrange("p (o t e) -> p o t e", o=half, e=2)
                    dst = aT[:, :, :].rearrange("p t (o g) -> p o t g", g=OG)
                    for e in range(2):
                        V.tensor_copy(dst[e * C:(e + 1) * C, h * half:(h + 1) * half, :, g],
                                      src[e * C:(e + 1) * C, :, :, e]).then_inc(s_aggv, 1)

            def agg_b(c):
                dve.wait_ge(s_bb, c + 1)
                V.tensor_copy(bbc[:, :], YB[1][:, :]).then_inc(s_bbv, 1)

            def conv(c, k):
                dve.wait_ge(s_y, KH * c + k + 1)
                if k == 0:
                    dve.wait_ge(s_bbv, c + 1)
                    if not (isinstance(c, int) and c == 0):
                        dve.wait_ge(s_yhi, KH * c)
                        dve.wait_ge(s_ylo, KH * c)
                V.tensor_tensor(ys[:, k, :], YB[k % 2][:, :], bbc[:, :], ALU.add).then_inc(s_yv, 1)
                if k >= 1:
                    add_l1(c, k - 1)
                if k == KH - 1:
                    add_l1(c, k)

            def add_l1(c, k):
                dve.wait_ge(s_abs, KH * c + k + 1)
                if k == 0:
                    if not (isinstance(c, int) and c == 0):
                        dve.wait_ge(s_norm, c)
                    V.tensor_copy(l1[:, :], ab[:, 0, :]).then_inc(s_l1, 1)
                else:
                    dve.wait_ge(s_l1, KH * c + k)
                    V.tensor_tensor(l1[:, :], l1[:, :], ab[:, k % 2, :], ALU.add).then_inc(s_l1, 1)

            def scales(c):
                dve.wait_ge(s_norm, c + 1)
                V.tensor_scalar(p2[:, :], YB[0][:, :], 2.0 ** -60, None, ALU.max).then_inc(s_pos, 1)
                dve.wait_ge(s_pos, c + 1)
                V.tensor_scalar(p2[:, :].bitcast(i32), p2[:, :].bitcast(i32), EXPONENT, None,
                                ALU.bitwise_and).then_inc(s_p2, 1)
                dve.wait_ge(s_p2, c + 1)
                V.tensor_scalar(scl[:, :].bitcast(i32), p2[:, :].bitcast(i32), -1.0,
                                float((2 * 127 + L1_LOG) << 23), ALU.mult, ALU.add).then_inc(s_scl, 1)
                dve.wait_ge(s_scl, c + 1)
                for k in range(KH):
                    V.tensor_tensor(ys[:, k, :], ys[:, k, :], scl[:, :], ALU.mult).then_inc(s_ysc, 1)
                for k in range(KH):
                    dve.wait_ge(s_yhi, KH * c + k + 1)
                    V.tensor_tensor(yp[:, k, 1, :], ys[:, k, :], yp[:, k, 0, :], ALU.subtract).then_inc(s_ylo, 1)

            def out_scales(c):
                dve.wait_ge(s_p2T, c + 1)
                V.tensor_copy(p2t[:, :], YB[1][:, 0:NT]).then_inc(s_p2v, 1)

            def out_scales2(c):
                dve.wait_ge(s_p2v, c + 1)
                dve.wait_ge(s_kk, 3)
                V.scalar_tensor_tensor(osc[:, :], p2t[:, :], kk[:, 2:3], p2t[:, :],
                                       ALU.mult, ALU.mult).then_inc(s_osc, 1)

            def threshold(m, n):
                V.tensor_reduce(tot[:, m:m + 1], wsum[:, 0:n], AX.X, ALU.add).then_inc(s_tot, 1)
                dve.wait_ge(s_totm, m + 1)
                V.tensor_scalar(mean[:, m:m + 1], YB[0][:, 0:1], 1.0 / (F * H), None, ALU.mult).then_inc(s_mean, 1)
                dve.wait_ge(s_mean, m + 1)
                V.tensor_scalar(den[:, m:m + 1], mean[:, m:m + 1], EPS, None, ALU.add).then_inc(s_den, 1)
                dve.wait_ge(s_den, m + 1)
                V.tensor_scalar(nthr[:, m:m + 1], den[:, m:m + 1], -0.5, None, ALU.mult)
                V.tensor_scalar(thr[:, m:m + 1], den[:, m:m + 1], 0.5, None, ALU.mult).then_inc(s_thr, 1)

            def quantise(n):
                m, e = min(n // NG, 2), q_entry(n)
                rows, cols = raw[e][2:]
                if n in (0, NG, 2 * NG):
                    dve.wait_ge(s_thr, m + 1)
                raw_arrived(dve, e)
                dve.wait_ge(s_gt, n + 1)
                buf = msk[0:rows, n % 2, 0:cols]
                V.scalar_tensor_tensor(buf, ring[e % RING][0:rows, 0:cols], nthr[0:rows, m:m + 1], buf,
                                       ALU.is_lt, ALU.subtract).then_inc(s_q, 1)
                dve.wait_ge(s_q, n + 1)
                dve.sem_inc(s_raw_free["dve"], 1)

            def product(c, u):
                dve.wait_ge(s_gu, GU * c + FT + u + 1)
                if u >= 2:
                    dve.wait_ge(s_uhi, UP * c + u - 1)
                    dve.wait_ge(s_ulo, UP * c + u - 1)
                elif not (isinstance(c, int) and c == 0):
                    dve.wait_ge(s_uhi, UP * c)
                    dve.wait_ge(s_ulo, UP * c)
                bank = GUB[(FT + u) % 4]
                if u == 0:
                    dve.wait_ge(s_gr, c + 1)
                    V.scalar_tensor_tensor(prod[C:P, 0, :], bank[C:P, :], PROD, g_r[C:P, :],
                                           ALU.mult, ALU.mult).then_inc(s_uv, 1)
                else:
                    dve.wait_ge(s_gv, FT * c + u)
                    V.scalar_tensor_tensor(prod[:, u % 2, :], bank[:, :], PROD, inter[:, u - 1, :],
                                           ALU.mult, ALU.mult).then_inc(s_uv, 1)

            def split(c, u):
                if u == 0:
                    dve.wait_ge(s_hir, c + 1)
                    dve.wait_ge(s_uhi, UP * c + 1)
                    if not (isinstance(c, int) and c == 0):
                        dve.wait_ge(s_dn, DN * c)
                    V.tensor_tensor(inter_r[C:P, :], prod[C:P, 0, :], hi_r[C:P, :], ALU.subtract).then_inc(s_ulo, 1)
                else:
                    dve.wait_ge(s_uhi, UP * c + u + 1)
                    V.tensor_tensor(part(u - 1, 1), prod[:, u % 2, :], part(u - 1, 0),
                                    ALU.subtract).then_inc(s_ulo, 1)

            def output(c, d):
                t, n = d // HB, d % HB
                dve.wait_ge(s_dn, DN * c + d + 1)
                if n == 0:
                    dve.wait_ge(s_xr, NT * c + t + 1)
                cols = slice(n * TOK, (n + 1) * TOK)
                V.scalar_tensor_tensor(xr[:, t, cols], DNB[d % 2][:, :], osc[:, t:t + 1], xr[:, t, cols],
                                       ALU.mult, ALU.add).then_inc(s_o, 1)

            agg_b(0)
            for k in range(KH):
                conv(0, k)
            scales(0)
            out_scales(0)
            dve.wait_ge(s_raw_free["act"], NG)
            threshold(0, NG)
            for n in range(NG):
                quantise(n)
            for n in range(NG):
                e = U_SUM + n
                rows, cols = raw[e][2:]
                raw_arrived(dve, e)
                V.tensor_reduce(wsum[0:rows, n:n + 1], ring[e % RING][0:rows, 0:cols], AX.X, ALU.add,
                                apply_absolute_value=True).then_inc(s_usum, 1)
                dve.wait_ge(s_usum, n + 1)
                dve.sem_inc(s_raw_free["dve"], 1)
            threshold(1, NG)
            for n in range(NG, 2 * NG):
                quantise(n)
            at = [i for i, (what, _) in enumerate(order0) if what == "U"]
            t_dn = 2 * NG
            for u in range(UP):
                product(0, u)
                if u >= 1:
                    split(0, u - 1)
                if u == 8:
                    dve.wait_ge(s_raw_free["act"], NG + ND)
                    threshold(2, ND)
                if 8 <= u < 8 + ND // 2:
                    quantise(t_dn)
                    quantise(t_dn + 1)
                    t_dn += 2
            split(0, UP - 1)
            V.tensor_scalar(kk[:, 0:1], mean[:, 0:1], -(2.0 ** -(2 * L1_LOG)) / PROD, None, ALU.mult).then_inc(s_kk, 1)
            dve.wait_ge(s_kk, 1)
            V.tensor_tensor(kk[:, 1:2], kk[:, 0:1], mean[:, 1:2], ALU.mult).then_inc(s_kk, 1)
            dve.wait_ge(s_kk, 2)
            V.tensor_tensor(kk[:, 2:3], kk[:, 1:2], mean[:, 2:3], ALU.mult).then_inc(s_kk, 1)
            out_scales2(0)
            agg_b(1)
            for k in range(KH):
                conv(1, k)

            def outputs(c, more):
                if more:
                    scales(c + 1)
                for d in range(DN):
                    output(c, d)
                if more:
                    out_scales(c + 1)
                    out_scales2(c + 1)

            outputs(0, True)

            def chunk(c, more):
                for u in range(UP):
                    product(c, u)
                    if u >= 1:
                        split(c, u - 1)
                    if more and u == 11:
                        agg_b(c + 1)
                    if more and u - 12 in range(KH):
                        conv(c + 1, u - 12)
                split(c, UP - 1)
                outputs(c, more)

            with dve.Fori(1, NC - 1) as c:
                chunk(c, True)
            chunk(NC - 1, False)


_INS = ['x', 'cond_128', 'L0_cond_W0', 'L0_cond_b0', 'L0_cond_W1', 'L0_cond_b1', 'L0_cond_W2', 'L0_cond_b2',
        'L0_cond_weight', 'L0_cond_bias_k', 'L0_ffn_w_gate', 'L0_ffn_w_up', 'L0_ffn_w_down']
_OUTS = [((64, 64, 1024), 'float32')]


def kernel(**inputs):
    import numpy as _np
    import concourse.bacc as _bacc
    from concourse import mybir as _mybir
    from concourse.bass_utils import run_bass_kernel_spmd as _run

    nc = _bacc.Bacc("TRN2", target_bir_lowering=False, num_devices=1)
    arrays, args = {}, []
    for name in _INS:
        a = _np.ascontiguousarray(inputs[name])
        arrays[f"in_{name}_dram"] = a
        args.append(nc.dram_tensor(f"in_{name}_dram", a.shape, _mybir.dt.from_np(a.dtype), kind="ExternalInput").ap())
    for i, (shape, dtype) in enumerate(_OUTS):
        dt = _mybir.dt.from_np(_np.dtype(dtype))
        args.append(nc.dram_tensor(f"out_{i}_dram", shape, dt, kind="ExternalOutput").ap())
    adaln_ternary_ffn(nc, *args)
    r = _run(nc, [arrays], core_ids=[0])
    return r.results[0]["out_0_dram"]
```

```python
import concourse.bass as bass
from concourse import mybir
from contextlib import ExitStack


def adaln_ternary_ffn(nc: bass.Bass, x, cond, w0, b0, w1, b1, w2, b2, wk, bias_k, w_gate, w_up, w_down, out):
    f32, bf16, f16, f8, i32 = (mybir.dt.float32, mybir.dt.bfloat16, mybir.dt.float16,
                               mybir.dt.float8e4, mybir.dt.int32)
    ALU, ACT, AX = mybir.AluOpType, mybir.ActivationFunctionType, mybir.AxisListType

    P = 128
    B, C, H = x.shape
    F = w_gate.shape[0]
    NK = wk.shape[0]
    EPS = 1e-5
    TOK = 512
    NT = TOK // P
    NC = B * C // TOK
    BC = TOK // C
    KH = H // P
    FT = F // P
    FR = F - FT * P
    assert FR == 64 and C == 64
    GU = 2 * FT + 1
    UP = FT + 1
    HB = H // TOK
    DN = NT * HB
    OO = P // NK
    OG = C // OO
    CT = 1024
    DP = -(-F // CT)
    L1_LOG = 14
    PROD = 2.0 ** -15
    EXPONENT = 0x7F800000

    NG, ND = FT + 1, KH * DP
    NQ = 2 * NG + ND
    tiles = []
    for w in (w_gate, w_up):
        for f in range(NG):
            rows = min(P, F - f * P)
            tiles.append((w[f * P:f * P + rows, :], rows, H))
    for r in range(KH):
        for m in range(DP):
            cols = min(CT, F - m * CT)
            tiles.append((w_down[r * P:(r + 1) * P, m * CT:m * CT + cols], P, cols))

    SLOTS = ([("xr", t) for t in range(4)] + [("raw", 0)], [("wd", i) for i in range(5)],
             [("wu", i) for i in range(5)], [("inter", i) for i in range(3, 10)], [("ys", i) for i in range(4)])
    base, wd, wu, it, yy = SLOTS
    loads = []
    loads += [(n, True, True, s) for n, s in enumerate(wd + base + it + wu)]
    loads += [(NG + m, True, False, s) for m, s in zip((19, 20, 21), wd)]
    held = wd[3:] + base + wd[:3] + yy + [("prod", 0)] + it[3:]
    loads += [(NG + m, True, True, s) for m, s in zip([*range(4, 19), *range(4)], held)]
    loads += [(NG + m, False, True, s) for m, s in zip((19, 20, 21), held)]
    HOLD = 9
    loads += [(2 * NG + n, True, False, (base[1:] + wd[:3])[i % 7]) for i, n in enumerate(range(HOLD, ND))]
    loads += [(2 * NG + n, True, True, s) for n, s in enumerate(base + yy)]
    loads += [(2 * NG + n, False, True, (base + yy)[(n - HOLD) % HOLD]) for n in range(HOLD, ND)]
    summed = [e for e, (n, s, _, _) in enumerate(loads) if s]
    q_load = {n: e for e, (n, _, q, _) in enumerate(loads) if q}
    assert len(summed) == NQ and sorted(q_load) == list(range(NQ))
    on_act = [i < NG or i % 2 == 0 for i in range(NQ)]

    def sum_count(i):
        return on_act[i], sum(on_act[k] == on_act[i] for k in range(i + 1))

    order0 = [("T", 0), ("T", 1)]
    nt, ns = 2, NG
    for f in range(FT):
        order0.append(("G", f))
        if f < 10:
            for _ in range((1, 2, 2, 2, 2, 2, 2, 3, 3, 3)[f]):
                order0.append(("S", ns))
                ns += 1
        if f >= 14:
            for _ in range(2):
                order0.append(("S", ns))
                ns += 1
        for _ in range(2):
            order0.append(("T", nt))
            nt += 1
    assert nt == 2 * NG
    for u in range(UP):
        order0.append(("U", u))
        if u < 2:
            for _ in range(5):
                order0.append(("S", ns))
                ns += 1
        if u == 1:
            order0.append(("D", 0))
        if u >= 2 and nt < NQ:
            for _ in range(2):
                order0.append(("T", nt))
                nt += 1
    assert nt == NQ and ns == NQ

    ctx = ExitStack()
    with ctx:
        def sb(name, shape, dt):
            return ctx.enter_context(nc.sbuf_tensor(name, shape, dt))

        def sem(name):
            return ctx.enter_context(nc.semaphore(name))

        wgT = sb("wgT", [P, KH, FT * P], f8)
        wuT = sb("wuT", [P, KH, FT * P], f8)
        wrT = sb("wrT", [P, KH, 2 * FR], f8)
        wdT = sb("wdT", [P, FT + 1, H], f8)
        inter = sb("inter", [P, FT, TOK], f32)
        inter_r = sb("inter_r", [P, TOK], f16)
        yp = sb("yp", [P, KH, 2, TOK], f16)
        ys = sb("ys", [P, KH, TOK], f32)
        xa = sb("xa", [P, NT, H], f32)
        xr = sb("xr", [P, NT, H], f32)
        aT = sb("aT", [P, B // 2, C], f32)
        ablk = sb("ablk", [P, NT, P], f32)
        bprod = sb("bprod", [NK, TOK], f32)
        bbc = sb("bbc", [P, TOK], f32)
        prod = sb("prod", [P, 2, TOK], f32)
        g_r = sb("g_r", [P, TOK], f32)
        hi_r = sb("hi_r", [P, TOK], f16)
        ab = sb("ab", [P, 2, TOK], bf16)
        l1 = sb("l1", [P, TOK], bf16)
        p2 = sb("p2", [P, TOK], f32)
        p2b = l1[0:1, :]
        scl = bbc
        raw5 = sb("raw5", [P, CT], f32)
        msk = sb("msk", [P, 2, CT], bf16)
        identb = sb("identb", [P, P], bf16)
        onesb = sb("onesb", [P, P], bf16)
        ones = sb("ones", [P, P], f32)
        attT = sb("attT", [NK, B], f32)
        biask = sb("biask", [NK, C], f32)
        wsum = sb("wsum", [P, ND], f32)
        tot = sb("tot", [P, 3], f32)
        mean = sb("mean", [P, 3], f32)
        den = sb("den", [P, 3], f32)
        thr = sb("thr", [P, 3], f32)
        nthr = sb("nthr", [P, 3], f32)
        kk = sb("kk", [P, 3], f32)
        p2t = sb("p2t", [P, NT], f32)
        osc = sb("osc", [P, NT], f32)

        def slot(which, i):
            if which == "xr":
                return xr[:, i, :]
            if which == "raw":
                return raw5[:, :]
            if which == "prod":
                return prod[:, :, :].rearrange("p a n -> p (a n)")
            if which == "inter":
                return inter[:, 2 * i:2 * i + 2, :].rearrange("p a n -> p (a n)")
            if which == "ys":
                return ys[:, 2 * i:2 * i + 2, :].rearrange("p a n -> p (a n)")
            w = {"wu": wuT, "wd": wdT}[which][:, :, :].rearrange("p a n -> p (a n)")
            return w[:, i * 4 * CT:(i + 1) * 4 * CT].bitcast(f32)

        def raw(e):
            n, _, _, s = loads[e]
            return slot(*s)[0:tiles[n][1], 0:tiles[n][2]]

        def part(f, i):
            return inter[:, f, :].bitcast(f16)[:, i * TOK:(i + 1) * TOK]


        def early(n):
            return inter[:, n, :]
        w0_sb, w1_sb = early(0)[:, 0:P], early(0)[:, P:2 * P]
        w2_sb = early(0)[:, 2 * P:2 * P + NK]
        b0_sb, b1_sb = early(0)[:, 272:273], early(0)[:, 273:274]
        b2_sb = early(0)[0:B, 280:280 + NK]
        lg = early(0)[0:B, 290:290 + NK]
        ex = early(0)[0:B, 300:300 + NK]
        att = early(0)[0:B, 310:310 + NK]
        nmx, esum, rsum = (early(0)[0:B, 320 + i:321 + i] for i in range(3))
        mask = early(0)[:, 330:330 + OO]
        cond_sb, condT = early(1)[0:B, 0:P], early(1)[:, P:P + B]
        h1, h2 = early(1)[:, 192:192 + B], early(1)[:, 256:256 + B]
        attr = early(1)[0:B, 320:320 + P]
        attrT = early(1)[:, 448:448 + B]
        ident = early(2)[:, 0:P]
        wk_sb = inter[:, 3, :].rearrange("p (g d i) -> p g d i", g=OG, d=2)
        attd = inter[:, 4:6, :].rearrange("p h (o b) -> p h o b", b=B // 2)

        def agg_copy(copy, h, g, e):
            half = B // 4
            src = ps[OG * h + g][:, :].rearrange("p (o t e) -> p o t e", o=OO, e=2)
            dst = aT[:, :, :].rearrange("p t (o g) -> p o t g", g=OG)
            return copy(dst[e * C:(e + 1) * C, :, h * half:(h + 1) * half, g], src[e * C:(e + 1) * C, :, :, e])

        ps = [ctx.enter_context(nc.psum_tensor(f"ps{i}", [P, TOK], f32)) for i in range(8)]
        GUB, DNB, YB = ps[0:4], ps[4:6], ps[6:8]
        psb = [p[:, :].bitcast(bf16) for p in ps]

        s_cond = sem("s_cond")
        s_cond2 = sem("s_cond2")
        s_ident0 = sem("s_ident0")
        s_ident = sem("s_ident")
        s_pe = sem("s_pe")
        s_cv = sem("s_cv")
        s_ca = sem("s_ca")
        s_agg = sem("s_agg")
        s_aggv = sem("s_aggv")
        s_agga = sem("s_agga")
        slots = sorted({s for _, _, _, s in loads})
        s_raw = {s: sem(f"s_raw_{s[0]}{s[1]}") for s in slots}
        s_sum_act = sem("s_sum_act")
        s_sum_dve = sem("s_sum_dve")
        s_tot = sem("s_tot")
        s_totm = sem("s_totm")
        s_mean, s_den, s_thr = sem("s_mean"), sem("s_den"), sem("s_thr")
        s_gt = sem("s_gt")
        s_gtv = sem("s_gtv")
        s_q = sem("s_q")
        s_t = sem("s_t")
        s_te = sem("s_te")
        s_x = sem("s_x")
        s_xr = sem("s_xr")
        s_ablk = sem("s_ablk")
        s_bprod = sem("s_bprod")
        s_bb = sem("s_bb")
        s_bbv = sem("s_bbv")
        s_y = sem("s_y")
        s_yv = sem("s_yv")
        s_abs = sem("s_abs")
        s_l1 = sem("s_l1")
        s_norm = sem("s_norm")
        s_pos = sem("s_pos")
        s_p2 = sem("s_p2")
        s_p2b = sem("s_p2b")
        s_scl = sem("s_scl")
        s_p2T = sem("s_p2T")
        s_p2v = sem("s_p2v")
        s_osc = sem("s_osc")
        s_ysc = sem("s_ysc")
        s_yhi = sem("s_yhi")
        s_ylo = sem("s_ylo")
        s_gu = sem("s_gu")
        s_gv = sem("s_gv")
        s_gr = sem("s_gr")
        s_uv = sem("s_uv")
        s_hir = sem("s_hir")
        s_uhi = sem("s_uhi")
        s_ulo = sem("s_ulo")
        s_dn = sem("s_dn")
        s_o = sem("s_o")
        s_kk = sem("s_kk")
        s_turn_pe, s_turn_pool = sem("s_turn_pe"), sem("s_turn_pool")
        s_st = [sem(f"s_st{t}") for t in range(NT)]

        xt = x.rearrange("(t b) c h -> t (b c) h", b=2)
        ot = out.rearrange("(t b) c h -> t (b c) h", b=2)

        block = ctx.enter_context(nc.Block())

        @block.sync
        def _(sp):
            for i, (dst, src) in enumerate((
                    (cond_sb, cond), (w0_sb, w0), (b0_sb, b0[:, None]), (w1_sb, w1), (b1_sb, b1[:, None]),
                    (w2_sb, w2), (b2_sb, b2[None, :].broadcast_to([B, NK])), (biask[:, :], bias_k),
                    (wk_sb[:, :, 0, :], wk.rearrange("k (a g) i z -> (k a) g (i z)", g=OG)),
                    (wk_sb[:, :, 1, :], wk.rearrange("k (a g) i z -> (k a) g (i z)", g=OG)))):
                sp.dma_start(dst, src).then_inc(s_cond if i < 3 else s_cond2, 16)

            def load_x(c):
                sp.dma_start(xa[:, :, :], xt[bass.ds(c * NT, NT), :, :].rearrange("t p h -> p t h")).then_inc(s_x, 16)

            def store(c):
                for d in range(DN):
                    t, n = d // HB, d % HB
                    sp.wait_ge(s_o, DN * c + d + 1)
                    sp.dma_start(ot[c * NT + t, :, n * TOK:(n + 1) * TOK],
                                 xr[:, t, n * TOK:(n + 1) * TOK]).then_inc(s_st[t], 16)

            last_in = {}
            for e, (n, _, _, s) in enumerate(loads):
                if e == 8:
                    load_x(0)
                if s in last_in:
                    n0, _, quant, _ = loads[last_in[s]]
                    if quant:
                        sp.wait_ge(s_q, n0 + 1)
                    else:
                        act, count = sum_count(summed.index(last_in[s]))
                        sp.wait_ge(s_sum_act if act else s_sum_dve, count)
                elif s[0] == "ys":
                    sp.wait_ge(s_yhi, KH)
                    sp.wait_ge(s_ylo, KH)
                last_in[s] = e
                sp.dma_start(raw(e), tiles[n][0]).then_inc(s_raw[s], 16)

            sp.wait_ge(s_xr, NT)
            sp.wait_ge(s_y, KH)
            load_x(1)
            store(0)
            with sp.Fori(1, NC - 1) as c:
                sp.wait_ge(s_xr, NT * c + NT)
                sp.wait_ge(s_y, KH * c + KH)
                load_x(c + 1)
                store(c)
            store(NC - 1)
            for t in range(NT):
                sp.wait_ge(s_st[t], 16 * HB * NC)

        def raw_arrived(eng, e):
            s = loads[e][3]
            eng.wait_ge(s_raw[s], 16 * sum(x[3] == s for x in loads[:e + 1]))

        @block.gpsimd
        def _(pool):
            nc.gpsimd.memset(identb[:, :], 0.0).then_inc(s_ident0, 1)
            nc.gpsimd.memset(ident, 0.0).then_inc(s_ident0, 1)
            nc.gpsimd.memset(ones[:, :], 1.0)
            nc.gpsimd.memset(onesb[:, :], 1.0)
            nc.gpsimd.memset(wsum[:, :], 0.0)
            nc.gpsimd.memset(ablk[:, :, :], 0.0)
            pool.wait_ge(s_ident0, 2)
            for m in (ident, identb[:, :]):
                nc.gpsimd.affine_select(out=m, in_=m, compare_op=ALU.not_equal, fill=1.0, base=0,
                                        pattern=[[-1, P]], channel_multiplier=1).then_inc(s_ident, 1)
            def next_chunk(c):
                nc.gpsimd.tensor_tensor(
                    bprod[:, :].rearrange("k (b o) -> k b o", o=C),
                    attT[:, bass.ds(c * BC, BC)].unsqueeze(2).broadcast_to([NK, BC, C]),
                    biask[:, :].unsqueeze(1).broadcast_to([NK, BC, C]), ALU.mult).then_inc(s_bprod, 1)
                for h in range(2):
                    if h == 0:
                        pool.wait_ge(s_bprod, c + 1)
                        if isinstance(c, int) and c == 0:
                            pool.wait_ge(s_aggv, 2 * OG)
                            pool.wait_ge(s_agga, 2 * OG)
                    else:
                        pool.wait_ge(s_ablk, 2 * c + 1)
                    pool.sem_inc(s_turn_pool, 1)
                    nc.gpsimd.tensor_copy(ablk[h * C:(h + 1) * C, :, h * C:(h + 1) * C],
                                          aT[h * C:(h + 1) * C, bass.ds(c * NT, NT), :]).then_inc(s_ablk, 1)

            def residual(c):
                pool.wait_ge(s_x, 16 * (c + 1))
                pool.wait_ge(s_q, NQ)
                pool.sem_inc(s_turn_pool, 1)
                for t in range(NT):
                    nc.gpsimd.tensor_copy(xr[:, t, :], xa[:, t, :]).then_inc(s_xr, 1)

            pool.wait_ge(s_cv, 8)
            pool.wait_ge(s_cond2, 112)
            next_chunk(0)
            pool.wait_ge(s_ablk, 2)
            for n in range(0, NQ, 2):
                m = min(n // NG, 2)
                raw_arrived(pool, q_load[n])
                if n in (0, NG, 2 * NG):
                    pool.wait_ge(s_thr, m + 1)
                if n >= 2:
                    pool.wait_ge(s_t, n - 1)
                rows, cols = tiles[n][1:]
                nc.gpsimd.tensor_scalar(msk[0:rows, n % 2, 0:cols], raw(q_load[n]),
                                        thr[0:rows, m:m + 1], None, ALU.is_gt).then_inc(s_gt, 1)
            residual(0)

            def chunk(c):
                pool.wait_ge(s_y, KH * c + KH)
                pool.wait_ge(s_bb, c + 1)
                pool.wait_ge(s_xr, NT * c + NT)
                next_chunk(c + 1)
                pool.wait_ge(s_ablk, 2 * c + 4)
                for t in range(NT):
                    pool.wait_ge(s_st[t], 16 * HB * (c + 1))
                residual(c + 1)

            chunk(0)
            with pool.Fori(1, NC - 1) as c:
                chunk(c)

        @block.tensor
        def _(pe):
            def mm(o, l, r, start=True, stop=True):
                return nc.tensor.matmul(o, l, r, start=start, stop=stop)

            pe.wait_ge(s_ident, 2)
            pe.wait_ge(s_cond, 48)
            nc.tensor.transpose(ps[0][:, 0:B], cond_sb, ident[0:B, 0:B]).then_inc(s_pe, 1)
            pe.wait_ge(s_cv, 1)
            mm(ps[1][:, 0:B], w0_sb, condT).then_inc(s_pe, 1)
            pe.wait_ge(s_ca, 1)
            pe.wait_ge(s_cond2, 112)
            mm(ps[2][:, 0:B], w1_sb, h1).then_inc(s_pe, 1)
            pe.wait_ge(s_ca, 2)
            mm(ps[3][0:B, 0:NK], h2, w2_sb).then_inc(s_pe, 1)
            pe.wait_ge(s_cv, 6)
            nc.tensor.transpose(ps[4][0:NK, 0:B], att, ident[0:B, 0:B]).then_inc(s_pe, 1)
            pe.wait_ge(s_cv, 7)
            nc.tensor.transpose(ps[5][:, 0:B], attr, ident[0:B, 0:B]).then_inc(s_pe, 1)
            pe.wait_ge(s_cv, 11)
            for h in range(2):
                for g in range(OG):
                    mm(ps[OG * h + g][:, :], wk_sb[:, g, :, :].rearrange("p d i -> p (d i)"),
                       attd[:, h, :, :].rearrange("p o b -> p (o b)")).then_inc(s_agg, 1)

            def agg_b(c):
                pe.wait_ge(s_bprod, c + 1)
                if isinstance(c, int) and c == 0:
                    pe.wait_ge(s_aggv, 2 * OG)
                    pe.wait_ge(s_agga, 2 * OG)
                else:
                    pe.wait_ge(s_osc, c)
                mm(YB[1][:, :], ones[0:NK, :], bprod[:, :]).then_inc(s_bb, 1)

            def conv(c, k):
                if k == 0:
                    pe.wait_ge(s_x, 16 * (c + 1))
                    pe.wait_ge(s_ablk, 2 * (c + 1))
                if k == 1:
                    pe.wait_ge(s_bbv, c + 1)
                if k >= 2:
                    pe.wait_ge(s_yv, KH * c + k - 1)
                for t in range(NT):
                    last = mm(YB[k % 2][:, t * P:(t + 1) * P], xa[:, t, k * P:(k + 1) * P], ablk[:, t, :])
                last.then_inc(s_y, 1)

            def norms(c):
                pe.wait_ge(s_l1, KH * (c + 1))
                mm(YB[0][:, :], onesb[:, :], l1[:, :]).then_inc(s_norm, 1)

            def norms_T(c):
                pe.wait_ge(s_p2b, c + 1)
                for t in range(NT):
                    last = mm(YB[1][:, t:t + 1], p2b[0:1, t * P:(t + 1) * P], onesb[0:1, 0:1])
                last.then_inc(s_p2T, 1)

            def total(m):
                pe.wait_ge(s_tot, m + 1)
                pe.wait_ge(s_sum_act, sum(on_act[:(NG, 2 * NG, NQ)[m]]))
                if m == 0:
                    pe.wait_ge(s_pos, 1)
                else:
                    pe.wait_ge(s_mean, m)
                mm(YB[0][:, 0:1], ones[:, :], tot[:, m:m + 1]).then_inc(s_totm, 1)

            def transpose(n):
                rows, cols = tiles[n][1:]
                pe.wait_ge(s_q, n + 1)
                if n >= 2:
                    pe.wait_ge(s_te, n - 1)
                bank = psb[4 + n % 2]
                nb = -(-cols // P)
                for q in range(nb):
                    w = min(P, cols - q * P)
                    last = nc.tensor.transpose(bank[0:w, q * P:q * P + rows], msk[0:rows, n % 2, q * P:q * P + w],
                                               identb[0:rows, 0:rows])
                last.then_inc(s_t, 1)

            def waited(c):
                if not isinstance(c, int):
                    pe.sem_inc(s_turn_pe, 1)

            def group(c, j):
                if j < 4:
                    if not (isinstance(c, int) and c == 0):
                        pe.wait_ge(s_uv, UP * c)
                elif j - 4 < FT:
                    pe.wait_ge(s_gv, FT * c + j - 3)
                else:
                    pe.wait_ge(s_uv, UP * c + j - 3 - FT)
                waited(c)
                for k in range(KH):
                    if j == 0:
                        pe.wait_ge(s_ylo, KH * c + k + 1)
                        waited(c)
                    if j < FT:
                        w = wgT[:, k, j * P:(j + 1) * P]
                    elif j == FT:
                        w = wrT[:, k, :]
                    else:
                        w = wuT[:, k, (j - UP) * P:(j - UP + 1) * P]
                    for i in range(2):
                        last = mm(GUB[j % 4][:, :], w, yp[:, k, i, :], start=(k + i == 0), stop=(k == KH - 1 and i == 1))
                last.then_inc(s_gu, 1)

            def down(c, d):
                t, n = d // HB, d % HB
                if d >= 2:
                    pe.wait_ge(s_o, DN * c + d - 1)
                elif isinstance(c, int) and c == 0:
                    pe.wait_ge(s_te, NQ)
                else:
                    pe.wait_ge(s_o, DN * c)
                cols = slice(n * TOK, (n + 1) * TOK)
                if d == 0:
                    pe.wait_ge(s_ulo, UP * c + 1)
                waited(c)
                mm(DNB[d % 2][:, :], inter_r[:, t * P:(t + 1) * P], wdT[:, FT, cols], start=True, stop=False)
                for f in range(FT):
                    if d == 0:
                        pe.wait_ge(s_ulo, UP * c + f + 2)
                        waited(c)
                    for i in range(2):
                        last = mm(DNB[d % 2][:, :], part(f, i)[:, t * P:(t + 1) * P], wdT[:, f, cols],
                                  start=False, stop=(f == FT - 1 and i == 1))
                last.then_inc(s_dn, 1)

            def downs(c, more):
                for d in range(DN):
                    down(c, d)
                    if more and d == 0:
                        norms(c + 1)
                    if more and d == 1:
                        norms_T(c + 1)

            agg_b(0)
            for k in range(KH):
                conv(0, k)
            norms(0)
            norms_T(0)
            total(0)
            for what, n in order0:
                if what == "T":
                    if n == NG:
                        total(1)
                    transpose(n)
                elif what == "D":
                    total(2)
                elif what == "G":
                    if n == 0:
                        pe.wait_ge(s_te, 1)
                    else:
                        pe.wait_ge(s_te, n + 1)
                    group(0, n)
                elif what == "U":
                    pe.wait_ge(s_te, 2 * NG if n == 0 else NG + n)
                    group(0, FT + n)
            agg_b(1)
            for k in range(KH):
                conv(1, k)
            downs(0, True)

            def chunk(c, more):
                for j in range(GU):
                    group(c, j)
                    if more and j == UP + 9:
                        agg_b(c + 1)
                    if more and j - UP - 11 in range(KH):
                        conv(c + 1, j - UP - 11)
                downs(c, more)

            with pe.Fori(1, NC - 1) as c:
                chunk(c, True)
            chunk(NC - 1, False)

        @block.scalar
        def _(act):
            def magnitudes(c, k):
                act.wait_ge(s_yv, KH * c + k + 1)
                if k >= 2:
                    act.wait_ge(s_l1, KH * c + k - 1)
                elif not (isinstance(c, int) and c == 0):
                    act.wait_ge(s_l1, KH * c)
                nc.scalar.activation(ab[:, k % 2, :], ys[:, k, :], ACT.Abs).then_inc(s_abs, 1)

            def split_y(c):
                for k in range(KH):
                    act.wait_ge(s_ysc, KH * c + k + 1)
                    nc.scalar.copy(yp[:, k, 0, :], ys[:, k, :]).then_inc(s_yhi, 1)

            act.wait_ge(s_pe, 2)
            nc.scalar.activation(h1, ps[1][:, 0:B], ACT.Gelu, bias=b0_sb).then_inc(s_ca, 1)
            act.wait_ge(s_pe, 3)
            nc.scalar.activation(h2, ps[2][:, 0:B], ACT.Gelu, bias=b1_sb).then_inc(s_ca, 1)
            act.wait_ge(s_cv, 3)
            nc.scalar.activation(ex, lg, ACT.Exp, bias=nmx, accum_out=esum).then_inc(s_ca, 1)

            for h in range(2):
                for g in range(OG):
                    act.wait_ge(s_agg, OG * h + g + 1)
                    agg_copy(nc.scalar.copy, h, g, 1).then_inc(s_agga, 1)

            def raw_sum(i):
                e = summed[i]
                n = loads[e][0]
                rows, col = tiles[n][1], n - min(n // NG, 2) * NG
                if i == NG or i == 2 * NG:
                    act.wait_ge(s_tot, i // NG)
                raw_arrived(act, e)
                a, bufs = sum_count(i)[1], 2 if i < NG else 1
                if a > bufs:
                    act.wait_ge(s_sum_act, a - bufs)
                junk = msk[:, a % 2, :] if i < NG else g_r[:, :].bitcast(bf16)
                nc.scalar.activation(junk[0:rows, 0:tiles[loads[e][0]][2]], raw(e), ACT.Abs,
                                     accum_out=wsum[0:rows, col:col + 1]).then_inc(s_sum_act, 1)

            for n in range(NG):
                raw_sum(n)
                if n - 13 in range(KH):
                    magnitudes(0, n - 13)
            split_y(0)

            def copy_T(n):
                act.wait_ge(s_t, n + 1)
                bank = psb[4 + n % 2]
                if n < 2 * NG:
                    f = n % NG
                    if f < FT:
                        dst = (wgT, wuT)[n // NG][:, :, f * P:(f + 1) * P]
                        src = bank[:, 0:KH * P].rearrange("p (k f) -> p k f", f=P)
                    else:
                        dst = wrT[:, :, (n // NG) * FR:(n // NG + 1) * FR]
                        src = bank[:, 0:KH * P].rearrange("p (k f) -> p k f", f=P)[:, :, 0:FR]
                    nc.scalar.copy(dst, src, saturate=False).then_inc(s_te, 1)
                    return
                r, m = divmod(n - 2 * NG, DP)
                f0, nf = m * (CT // P), min(CT // P, FT - m * (CT // P))
                last = nc.scalar.copy(wdT[:, f0:f0 + nf, r * P:(r + 1) * P],
                                      bank[:, 0:nf * P].rearrange("p (f h) -> p f h", h=P), saturate=False)
                if f0 + nf == FT:
                    for h in range(2):
                        last = nc.scalar.copy(wdT[h * FR:(h + 1) * FR, FT, r * P:(r + 1) * P],
                                              bank[0:FR, nf * P:(nf + 1) * P], saturate=False)
                last.then_inc(s_te, 1)

            def gate(c, f):
                act.wait_ge(s_gu, GU * c + f + 1)
                if f == 0 and not (isinstance(c, int) and c == 0):
                    act.wait_ge(s_dn, DN * c)
                if isinstance(c, int) and c == 0:
                    for n, e in q_load.items():
                        if loads[e][3] == ("inter", f // 2):
                            act.wait_ge(s_q, n + 1)
                nc.scalar.copy(inter[:, f, :], GUB[f % 4][:, :]).then_inc(s_gv, 1)

            def up(c, u):
                if u == 0:
                    act.wait_ge(s_gu, GU * c + FT + 1)
                    if isinstance(c, int) and c == 0:
                        before = [n for what, n in order0[:order0.index(("U", 0))] if what == "S"]
                        act.wait_ge(s_sum_act, sum(on_act[:max(before) + 1]))
                    nc.scalar.copy(g_r[C:P, :], GUB[FT % 4][0:C, :]).then_inc(s_gr, 1)
                    act.wait_ge(s_uv, UP * c + 1)
                    nc.scalar.copy(hi_r[C:P, :], prod[C:P, 0, :]).then_inc(s_hir, 1)
                    nc.scalar.copy(inter_r[0:C, :], prod[C:P, 0, :]).then_inc(s_uhi, 1)
                else:
                    act.wait_ge(s_uv, UP * c + u + 1)
                    nc.scalar.copy(part(u - 1, 0), prod[:, u % 2, :]).then_inc(s_uhi, 1)

            for what, n in order0:
                if what == "T":
                    copy_T(n)
                elif what == "G":
                    gate(0, n)
                elif what == "U":
                    up(0, n)
                elif what == "S" and on_act[n]:
                    raw_sum(n)
            for k in range(KH):
                magnitudes(1, k)
            split_y(1)

            def chunk(c, more):
                for f in range(FT):
                    gate(c, f)
                for u in range(UP):
                    up(c, u)
                    if more and u - 12 in range(KH):
                        magnitudes(c + 1, u - 12)
                if more:
                    split_y(c + 1)

            with act.Fori(1, NC - 1) as c:
                chunk(c, True)
            chunk(NC - 1, False)

        @block.vector
        def _(dve):
            V = nc.vector
            dve.wait_ge(s_pe, 1)
            V.tensor_copy(condT, ps[0][:, 0:B]).then_inc(s_cv, 1)
            dve.wait_ge(s_pe, 4)
            V.tensor_tensor(lg, ps[3][0:B, 0:NK], b2_sb, ALU.add).then_inc(s_cv, 1)
            dve.wait_ge(s_cv, 2)
            V.tensor_reduce(nmx, lg, AX.X, ALU.max, negate=True).then_inc(s_cv, 1)
            dve.wait_ge(s_ca, 3)
            V.reciprocal(rsum, esum).then_inc(s_cv, 1)
            dve.wait_ge(s_cv, 4)
            V.tensor_scalar(att, ex, rsum, None, ALU.mult).then_inc(s_cv, 1)
            V.tensor_reduce(mask, ident.rearrange("p (k o) -> p o k", o=OO), AX.X, ALU.add).then_inc(s_cv, 1)
            dve.wait_ge(s_cv, 5)
            V.tensor_copy(attr.rearrange("b (k o) -> b k o", o=OO),
                          att.unsqueeze(2).broadcast_to([B, NK, OO])).then_inc(s_cv, 1)
            dve.wait_ge(s_pe, 5)
            V.tensor_copy(attT[:, :], ps[4][0:NK, 0:B]).then_inc(s_cv, 1)
            dve.wait_ge(s_pe, 6)
            V.tensor_copy(attrT, ps[5][:, 0:B]).then_inc(s_cv, 1)
            dve.wait_ge(s_cv, 9)
            for h in range(2):
                V.tensor_tensor(attd[:, h, :, :],
                                attrT[:, h * B // 2:(h + 1) * B // 2].unsqueeze(1).broadcast_to([P, OO, B // 2]),
                                mask.unsqueeze(2).broadcast_to([P, OO, B // 2]), ALU.mult).then_inc(s_cv, 1)
            for h in range(2):
                for g in range(OG):
                    dve.wait_ge(s_agg, OG * h + g + 1)
                    agg_copy(V.tensor_copy, h, g, 0).then_inc(s_aggv, 1)

            def agg_b(c):
                dve.wait_ge(s_bb, c + 1)
                V.tensor_copy(bbc[:, :], YB[1][:, :]).then_inc(s_bbv, 1)

            def conv(c, k):
                dve.wait_ge(s_y, KH * c + k + 1)
                if k == 0:
                    dve.wait_ge(s_bbv, c + 1)
                    if not (isinstance(c, int) and c == 0):
                        dve.wait_ge(s_yhi, KH * c)
                        dve.wait_ge(s_ylo, KH * c)
                V.tensor_tensor(ys[:, k, :], YB[k % 2][:, :], bbc[:, :], ALU.add).then_inc(s_yv, 1)
                if k >= 1:
                    add_l1(c, k - 1)
                if k == KH - 1:
                    add_l1(c, k)

            def add_l1(c, k):
                dve.wait_ge(s_abs, KH * c + k + 1)
                if k == 0:
                    if not (isinstance(c, int) and c == 0):
                        dve.wait_ge(s_norm, c)
                    V.tensor_copy(l1[:, :], ab[:, 0, :]).then_inc(s_l1, 1)
                else:
                    dve.wait_ge(s_l1, KH * c + k)
                    V.tensor_tensor(l1[:, :], l1[:, :], ab[:, k % 2, :], ALU.add).then_inc(s_l1, 1)

            def scales(c):
                dve.wait_ge(s_norm, c + 1)
                V.tensor_scalar(p2[:, :], YB[0][:, :], 2.0 ** -60, None, ALU.max).then_inc(s_pos, 1)
                dve.wait_ge(s_pos, c + 1)
                V.tensor_scalar(p2[:, :].bitcast(i32), p2[:, :].bitcast(i32), EXPONENT, None,
                                ALU.bitwise_and).then_inc(s_p2, 1)
                dve.wait_ge(s_p2, c + 1)
                V.tensor_scalar(scl[:, :].bitcast(i32), p2[:, :].bitcast(i32), -1.0,
                                float((2 * 127 + L1_LOG) << 23), ALU.mult, ALU.add).then_inc(s_scl, 1)
                V.tensor_copy(p2b[:, :], p2[0:1, :]).then_inc(s_p2b, 1)
                dve.wait_ge(s_scl, c + 1)

            def scale_y(c, k):
                V.tensor_tensor(ys[:, k, :], ys[:, k, :], scl[:, :], ALU.mult).then_inc(s_ysc, 1)

            def split_y(c, k):
                dve.wait_ge(s_yhi, KH * c + k + 1)
                V.tensor_tensor(yp[:, k, 1, :], ys[:, k, :], yp[:, k, 0, :], ALU.subtract).then_inc(s_ylo, 1)

            def out_scales(c):
                dve.wait_ge(s_p2T, c + 1)
                V.tensor_copy(p2t[:, :], YB[1][:, 0:NT]).then_inc(s_p2v, 1)

            def out_scales2(c):
                dve.wait_ge(s_p2v, c + 1)
                dve.wait_ge(s_kk, 3)
                V.scalar_tensor_tensor(osc[:, :], p2t[:, :], kk[:, 2:3], p2t[:, :],
                                       ALU.mult, ALU.mult).then_inc(s_osc, 1)

            def threshold(m, n):
                i = (NG, 2 * NG, NQ)[m]
                dve.wait_ge(s_sum_act, sum(on_act[:i]))
                if m:
                    dve.wait_ge(s_sum_dve, i - sum(on_act[:i]))
                V.tensor_reduce(tot[:, m:m + 1], wsum[:, 0:n], AX.X, ALU.add).then_inc(s_tot, 1)
                dve.wait_ge(s_totm, m + 1)
                V.tensor_scalar(mean[:, m:m + 1], YB[0][:, 0:1], 1.0 / (F * H), None, ALU.mult).then_inc(s_mean, 1)
                dve.wait_ge(s_mean, m + 1)
                V.tensor_scalar(den[:, m:m + 1], mean[:, m:m + 1], EPS, None, ALU.add).then_inc(s_den, 1)
                dve.wait_ge(s_den, m + 1)
                V.tensor_scalar(nthr[:, m:m + 1], den[:, m:m + 1], -0.5, None, ALU.mult)
                V.tensor_scalar(thr[:, m:m + 1], den[:, m:m + 1], 0.5, None, ALU.mult).then_inc(s_thr, 1)
                dve.wait_ge(s_thr, m + 1)

            def quantise(n):
                m, e = min(n // NG, 2), q_load[n]
                rows, cols = tiles[n][1:]
                buf = msk[0:rows, n % 2, 0:cols]
                if n % 2:
                    raw_arrived(dve, e)
                    if n >= 2:
                        dve.wait_ge(s_t, n - 1)
                    V.tensor_scalar(buf, raw(e), thr[0:rows, m:m + 1], None, ALU.is_gt).then_inc(s_gtv, 1)
                    dve.wait_ge(s_gtv, n // 2 + 1)
                else:
                    dve.wait_ge(s_gt, n // 2 + 1)
                V.scalar_tensor_tensor(buf, raw(e), nthr[0:rows, m:m + 1], buf,
                                       ALU.is_lt, ALU.subtract).then_inc(s_q, 1)

            def raw_sum(i):
                e = summed[i]
                n = loads[e][0]
                rows, col = tiles[n][1], n - min(n // NG, 2) * NG
                raw_arrived(dve, e)
                V.tensor_reduce(wsum[0:rows, col:col + 1], raw(e), AX.X, ALU.add,
                                apply_absolute_value=True).then_inc(s_sum_dve, 1)

            def product(c, u):
                dve.wait_ge(s_gu, GU * c + FT + u + 1)
                if u >= 2:
                    dve.wait_ge(s_uhi, UP * c + u - 1)
                    dve.wait_ge(s_ulo, UP * c + u - 1)
                elif not (isinstance(c, int) and c == 0):
                    dve.wait_ge(s_uhi, UP * c)
                    dve.wait_ge(s_ulo, UP * c)
                bank = GUB[(FT + u) % 4]
                if u == 0:
                    dve.wait_ge(s_gr, c + 1)
                    V.scalar_tensor_tensor(prod[C:P, 0, :], bank[C:P, :], PROD, g_r[C:P, :],
                                           ALU.mult, ALU.mult).then_inc(s_uv, 1)
                else:
                    dve.wait_ge(s_gv, FT * c + u)
                    V.scalar_tensor_tensor(prod[:, u % 2, :], bank[:, :], PROD, inter[:, u - 1, :],
                                           ALU.mult, ALU.mult).then_inc(s_uv, 1)

            def split(c, u):
                if u == 0:
                    dve.wait_ge(s_hir, c + 1)
                    dve.wait_ge(s_uhi, UP * c + 1)
                    if not (isinstance(c, int) and c == 0):
                        dve.wait_ge(s_dn, DN * c)
                    V.tensor_tensor(inter_r[C:P, :], prod[C:P, 0, :], hi_r[C:P, :], ALU.subtract).then_inc(s_ulo, 1)
                else:
                    dve.wait_ge(s_uhi, UP * c + u + 1)
                    V.tensor_tensor(part(u - 1, 1), prod[:, u % 2, :], part(u - 1, 0),
                                    ALU.subtract).then_inc(s_ulo, 1)

            def output(c, d):
                t, n = d // HB, d % HB
                dve.wait_ge(s_dn, DN * c + d + 1)
                if n == 0:
                    dve.wait_ge(s_xr, NT * c + t + 1)
                cols = slice(n * TOK, (n + 1) * TOK)
                V.scalar_tensor_tensor(xr[:, t, cols], DNB[d % 2][:, :], osc[:, t:t + 1], xr[:, t, cols],
                                       ALU.mult, ALU.add).then_inc(s_o, 1)

            agg_b(0)
            for k in range(KH):
                conv(0, k)
            scales(0)
            threshold(0, NG)
            for k in range(KH):
                scale_y(0, k)
                if k == 1:
                    quantise(0)
                if k == 5:
                    quantise(1)
                if k >= 2:
                    split_y(0, k - 2)
            split_y(0, KH - 2)
            split_y(0, KH - 1)
            out_scales(0)
            for what, n in order0:
                if what == "T" and n + 2 == NG:
                    threshold(1, NG)
                if what == "T" and (n + 2 < 2 * NG or 2 * NG <= n < NQ - 2):
                    quantise(n + 2)
                if what == "S" and not on_act[n]:
                    raw_sum(n)
                if what == "D":
                    threshold(2, ND)
                    quantise(2 * NG)
                    quantise(2 * NG + 1)
                if what == "U":
                    product(0, n)
                    if n >= 1:
                        split(0, n - 1)
            split(0, UP - 1)
            V.tensor_scalar(kk[:, 0:1], mean[:, 0:1], -(2.0 ** -(2 * L1_LOG)) / PROD, None, ALU.mult).then_inc(s_kk, 1)
            dve.wait_ge(s_kk, 1)
            V.tensor_tensor(kk[:, 1:2], kk[:, 0:1], mean[:, 1:2], ALU.mult).then_inc(s_kk, 1)
            dve.wait_ge(s_kk, 2)
            V.tensor_tensor(kk[:, 2:3], kk[:, 1:2], mean[:, 2:3], ALU.mult).then_inc(s_kk, 1)
            out_scales2(0)
            agg_b(1)
            for k in range(KH):
                conv(1, k)

            def outputs(c, more):
                output(c, 0)
                if more:
                    scales(c + 1)
                    for k in range(KH):
                        scale_y(c + 1, k)
                for d in range(1, DN):
                    output(c, d)
                    if more:
                        split_y(c + 1, d - 1)
                if more:
                    split_y(c + 1, KH - 1)
                    out_scales(c + 1)
                    out_scales2(c + 1)

            outputs(0, True)

            def chunk(c, more):
                for u in range(UP):
                    product(c, u)
                    if u >= 1:
                        split(c, u - 1)
                    if more and u == 11:
                        agg_b(c + 1)
                    if more and u - 12 in range(KH):
                        conv(c + 1, u - 12)
                split(c, UP - 1)
                outputs(c, more)

            with dve.Fori(1, NC - 1) as c:
                chunk(c, True)
            chunk(NC - 1, False)


_INS = ['x', 'cond_128', 'L0_cond_W0', 'L0_cond_b0', 'L0_cond_W1', 'L0_cond_b1', 'L0_cond_W2', 'L0_cond_b2',
        'L0_cond_weight', 'L0_cond_bias_k', 'L0_ffn_w_gate', 'L0_ffn_w_up', 'L0_ffn_w_down']
_OUTS = [((64, 64, 1024), 'float32')]


def kernel(**inputs):
    import numpy as _np
    import concourse.bacc as _bacc
    from concourse import mybir as _mybir
    from concourse.bass_utils import run_bass_kernel_spmd as _run

    nc = _bacc.Bacc("TRN2", target_bir_lowering=False, num_devices=1)
    arrays, args = {}, []
    for name in _INS:
        a = _np.ascontiguousarray(inputs[name])
        arrays[f"in_{name}_dram"] = a
        args.append(nc.dram_tensor(f"in_{name}_dram", a.shape, _mybir.dt.from_np(a.dtype), kind="ExternalInput").ap())
    for i, (shape, dtype) in enumerate(_OUTS):
        dt = _mybir.dt.from_np(_np.dtype(dtype))
        args.append(nc.dram_tensor(f"out_{i}_dram", shape, dt, kind="ExternalOutput").ap())
    adaln_ternary_ffn(nc, *args)
    r = _run(nc, [arrays], core_ids=[0])
    return r.results[0]["out_0_dram"]
```

```python
import concourse.bass as bass
from concourse import mybir
from contextlib import ExitStack


def adaln_ternary_ffn(nc: bass.Bass, x, cond, w0, b0, w1, b1, w2, b2, wk, bias_k, w_gate, w_up, w_down, out):
    f32, bf16, f16, f8, i32 = (mybir.dt.float32, mybir.dt.bfloat16, mybir.dt.float16,
                               mybir.dt.float8e4, mybir.dt.int32)
    ALU, ACT, AX = mybir.AluOpType, mybir.ActivationFunctionType, mybir.AxisListType

    P = 128
    B, C, H = x.shape
    F = w_gate.shape[0]
    NK = wk.shape[0]
    EPS = 1e-5
    TOK = 512
    NT = TOK // P
    NC = B * C // TOK
    BC = TOK // C
    KH = H // P
    FT = F // P
    FR = F - FT * P
    assert FR == 64 and C == 64
    GU = 2 * FT + 1
    UP = FT + 1
    HB = H // TOK
    DN = NT * HB
    OO = P // NK
    OG = C // OO
    CT = 1024
    DP = -(-F // CT)
    L1_LOG = 14
    PROD = 2.0 ** -15
    EXPONENT = 0x7F800000

    NG, ND = FT + 1, KH * DP
    NQ = 2 * NG + ND
    tiles = []
    for w, order in ((w_gate, range(NG)), (w_up, [FT, *range(FT)])):
        for f in order:
            rows = min(P, F - f * P)
            tiles.append((w[f * P:f * P + rows, :], rows, H))
    for r in range(KH):
        for m in range(DP):
            cols = min(CT, F - m * CT)
            tiles.append((w_down[r * P:(r + 1) * P, m * CT:m * CT + cols], P, cols))

    SLOTS = ([("xr", t) for t in range(4)] + [("raw", 0)], [("wd", i) for i in range(5)],
             [("wu", i) for i in range(5)], [("inter", i) for i in range(3, 10)], [("ys", i) for i in range(4)])
    base, wd, wu, it, yy = SLOTS
    loads = []
    loads += [(n, True, True, s) for n, s in enumerate(wd + base + it + wu)]
    loads += [(NG + m, True, False, s) for m, s in zip((19, 20, 21), wd)]
    held = wd[3:] + base + wd[:3] + yy + [("prod", 0)] + it[3:]
    loads += [(NG + m, True, True, s) for m, s in zip([*range(4, 19), *range(4)], held)]
    loads += [(NG + m, False, True, s) for m, s in zip((19, 20, 21), held)]
    HOLD = 9
    loads += [(2 * NG + n, True, False, (base[1:] + wd[:3])[i % 7]) for i, n in enumerate(range(HOLD, ND))]
    last = yy + [base[4], base[3], base[1], base[2], base[0]]
    loads += [(2 * NG + n, True, True, s) for n, s in enumerate(last)]
    loads += [(2 * NG + n, False, True, last[(n - HOLD) % HOLD]) for n in range(HOLD, ND)]

    def hidden(n):
        return n if n < NG else (n - 1) % NG

    summed = [e for e, (n, s, _, _) in enumerate(loads) if s]
    q_load = {n: e for e, (n, _, q, _) in enumerate(loads) if q}
    assert len(summed) == NQ and sorted(q_load) == list(range(NQ))
    SUM_DVE = (0, 1, 7, 10, 17, 21)
    on_act = [i not in SUM_DVE if i < NG else i % 4 != 1 if i < 2 * NG else
              i % 3 != 1 if i < 2 * NG + 12 else i % 2 == 0 for i in range(NQ)]

    def sum_count(i):
        return on_act[i], sum(on_act[k] == on_act[i] for k in range(i + 1))

    NM = 4
    SCD = 3

    order0 = [("T", 0), ("T", 1)]
    nt, ns = 2, NG

    def extend(what, first, count):
        order0.extend((what, first + i) for i in range(count))
        return first + count

    for f in range(FT):
        order0.append(("G", f))
        if f < 11:
            ns = extend("S", ns, 1 if f == 0 else 3 if f == 9 else 2)
        if f == 10:
            order0.append(("M", 1))
        elif f == 11:
            order0.append(("W", 1))
            extend("Q", NG + 1, NM - 1)
        nt = extend("T", nt, 1 if f in (0, 10) else 0 if f == 11 else 2)
        if f >= 15:
            ns = extend("S", ns, 2)
    for u in range(UP):
        order0.append(("U", u))
        ns = extend("S", ns, min(4, NQ - ns))
        if u == 2:
            order0.append(("M", 2))
        if u == 3:
            order0.append(("W", 2))
        if u == 4:
            extend("Q", 2 * NG + 1, NM - 1)
        nt = extend("T", nt, min(1 if u < 4 else 1 + u % 2, (2 * NG if u < 4 else NQ) - nt))
    assert nt == NQ and ns == NQ

    ctx = ExitStack()
    with ctx:
        def sb(name, shape, dt):
            return ctx.enter_context(nc.sbuf_tensor(name, shape, dt))

        def sem(name):
            return ctx.enter_context(nc.semaphore(name))

        wgT = sb("wgT", [P, KH, FT * P], f8)
        wuT = sb("wuT", [P, KH, FT * P], f8)
        wrT = sb("wrT", [P, KH, 2 * FR], f8)
        wdT = sb("wdT", [P, FT + 1, H], f8)
        inter = sb("inter", [P, FT, TOK], f32)
        inter_r = sb("inter_r", [P, TOK], f16)
        yp = sb("yp", [P, KH, 2, TOK], f16)
        ys = sb("ys", [P, KH, TOK], f32)
        xa = sb("xa", [P, NT, H], f32)
        xr = sb("xr", [P, NT, H], f32)
        aT = sb("aT", [P, B // 2, C], f32)
        ablk = sb("ablk", [P, NT, P], f32)
        bprod = sb("bprod", [NK, TOK], f32)
        bbc = sb("bbc", [P, TOK], f32)
        prod = sb("prod", [P, 2, TOK], f32)
        g_r = sb("g_r", [P, TOK], f32)
        hi_r = sb("hi_r", [P, TOK], f16)
        ab = sb("ab", [P, 2, TOK], bf16)
        l1 = sb("l1", [P, TOK], bf16)
        p2 = sb("p2", [P, TOK], f32)
        p2b = l1[0:1, :]
        scl = bbc
        raw5 = sb("raw5", [P, CT], f32)
        msk = sb("msk", [P, NM, CT], f8)
        gts = [ab[:, :, :].rearrange("p a n -> p (a n)"), bbc[:, :].bitcast(bf16)]
        junk = msk[:, :, :].rearrange("p m n -> p (m n)").bitcast(bf16)
        identb = sb("identb", [P, P], bf16)
        onesb = sb("onesb", [P, P], bf16)
        ones = sb("ones", [P, P], f32)
        attT = sb("attT", [NK, B], f32)
        biask = sb("biask", [NK, C], f32)
        wsum = sb("wsum", [P, ND], f32)
        tot = sb("tot", [P, 3], f32)
        mean = sb("mean", [P, 3], f32)
        thr = sb("thr", [P, 3], f32)
        nthr = sb("nthr", [P, 3], f32)
        kk = sb("kk", [P, 3], f32)
        p2t = sb("p2t", [P, NT], f32)
        osc = sb("osc", [P, NT], f32)

        def slot(which, i):
            if which == "xr":
                return xr[:, i, :]
            if which == "raw":
                return raw5[:, :]
            if which == "prod":
                return prod[:, :, :].rearrange("p a n -> p (a n)")
            if which == "inter":
                return inter[:, 2 * i:2 * i + 2, :].rearrange("p a n -> p (a n)")
            if which == "ys":
                return ys[:, 2 * i:2 * i + 2, :].rearrange("p a n -> p (a n)")
            w = {"wu": wuT, "wd": wdT}[which][:, :, :].rearrange("p a n -> p (a n)")
            return w[:, i * 4 * CT:(i + 1) * 4 * CT].bitcast(f32)

        def raw(e):
            n, _, _, s = loads[e]
            return slot(*s)[0:tiles[n][1], 0:tiles[n][2]]

        def part(f, i):
            return inter[:, f, :].bitcast(f16)[:, i * TOK:(i + 1) * TOK]


        def early(n):
            return inter[:, n, :]
        w0_sb, w1_sb = early(0)[:, 0:P], early(0)[:, P:2 * P]
        w2_sb = early(0)[:, 2 * P:2 * P + NK]
        b0_sb, b1_sb = early(0)[:, 272:273], early(0)[:, 273:274]
        b2_sb = early(0)[0:B, 280:280 + NK]
        lg = early(0)[0:B, 290:290 + NK]
        ex = early(0)[0:B, 300:300 + NK]
        att = early(0)[0:B, 310:310 + NK]
        nmx, esum, rsum = (early(0)[0:B, 320 + i:321 + i] for i in range(3))
        mask = early(0)[:, 330:330 + OO]
        cond_sb, condT = early(1)[0:B, 0:P], early(1)[:, P:P + B]
        h1, h2 = early(1)[:, 192:192 + B], early(1)[:, 256:256 + B]
        attr = early(1)[0:B, 320:320 + P]
        attrT = early(1)[:, 448:448 + B]
        ident = early(2)[:, 0:P]
        wk_sb = inter[:, 3, :].rearrange("p (g d i) -> p g d i", g=OG, d=2)
        attd = inter[:, 4:6, :].rearrange("p h (o b) -> p h o b", b=B // 2)

        def agg_copy(h, g):
            half = B // 4
            src = ps[g][:, :].rearrange("p (o t e) -> p o t e", o=OO, e=2)
            dst = aT[:, :, :].rearrange("p t (o g) -> p o t g", g=OG)
            for e in range(2):
                nc.vector.tensor_copy(dst[e * C:(e + 1) * C, :, h * half:(h + 1) * half, g],
                                      src[e * C:(e + 1) * C, :, :, e]).then_inc(s_aggv, 1)

        def block_diagonal(eng, c, h):
            return eng.tensor_copy(ablk[h * C:(h + 1) * C, :, h * C:(h + 1) * C],
                                   aT[h * C:(h + 1) * C, bass.ds(c * NT, NT), :]).then_inc(s_ablk, 1)

        ps = [ctx.enter_context(nc.psum_tensor(f"ps{i}", [P, TOK], f32)) for i in range(8)]
        GUB, DNB, YB = ps[0:4], ps[4:6], ps[6:8]
        psb = [p[:, :].bitcast(bf16) for p in ps]
        ps8 = [p[:, :].bitcast(f8) for p in ps]

        def quantised(n):
            rows, cols = tiles[n][1:]
            src, buf = raw(q_load[n]), msk[0:rows, n % NM, :]
            both = cols // (2 * P) * 2 * P
            parts = [(src[:, 0:both].rearrange("p (i c) -> p i c", i=2),
                      buf[:, 0:both].rearrange("p (c i) -> p i c", i=2))]
            if cols > both:
                parts.append((src[:, both:cols], buf[:, both:2 * cols - both].rearrange("p (c i) -> p i c", i=2)[:, 0, :]))
            if n % 2 == 0:
                return [(x, y, y) for x, y in parts]
            gt = gts[n // 2 % 2][0:rows, :]
            gt = [gt[:, 0:both].rearrange("p (i c) -> p i c", i=2), gt[:, both:cols]]
            return [(x, y, z) for (x, z), y in zip(parts, gt)]

        s_cond = sem("s_cond")
        s_cond2 = sem("s_cond2")
        s_cond3 = sem("s_cond3")
        s_ident0 = sem("s_ident0")
        s_ident = sem("s_ident")
        s_pe = sem("s_pe")
        s_cv = sem("s_cv")
        s_ca = sem("s_ca")
        s_agg = sem("s_agg")
        s_aggv = sem("s_aggv")
        slots = sorted({s for _, _, _, s in loads})
        s_raw = {s: sem(f"s_raw_{s[0]}{s[1]}") for s in slots}
        s_sum_act = sem("s_sum_act")
        s_sum_dve = sem("s_sum_dve")
        s_tot = sem("s_tot")
        s_totm = sem("s_totm")
        s_mean = sem("s_mean")
        s_thr = sem("s_thr")
        s_gt = sem("s_gt")
        s_gtv = sem("s_gtv")
        s_q = sem("s_q")
        s_t = sem("s_t")
        s_te = sem("s_te")
        s_x = sem("s_x")
        s_xr = sem("s_xr")
        s_ablk = sem("s_ablk")
        s_bprod = sem("s_bprod")
        s_bb = sem("s_bb")
        s_bbv = sem("s_bbv")
        s_y = sem("s_y")
        s_yv = sem("s_yv")
        s_abs = sem("s_abs")
        s_l1 = sem("s_l1")
        s_norm = sem("s_norm")
        s_pos = sem("s_pos")
        s_p2 = sem("s_p2")
        s_p2b = sem("s_p2b")
        s_scl = sem("s_scl")
        s_p2T = sem("s_p2T")
        s_p2v = sem("s_p2v")
        s_osc = sem("s_osc")
        s_ysc = sem("s_ysc")
        s_yscp = sem("s_yscp")
        s_yhi = sem("s_yhi")
        s_ylo = sem("s_ylo")
        s_gu = sem("s_gu")
        s_gv = sem("s_gv")
        s_gr = sem("s_gr")
        s_uv = sem("s_uv")
        s_hir = sem("s_hir")
        s_uhi = sem("s_uhi")
        s_ulo = sem("s_ulo")
        s_dn = sem("s_dn")
        s_o = sem("s_o")
        s_kk = sem("s_kk")
        s_turn_pe, s_turn_pool = sem("s_turn_pe"), sem("s_turn_pool")
        s_st = [sem(f"s_st{t}") for t in range(NT)]

        xt = x.rearrange("(t b) c h -> t (b c) h", b=2)
        ot = out.rearrange("(t b) c h -> t (b c) h", b=2)

        block = ctx.enter_context(nc.Block())

        @block.sync
        def _(sp):
            small = {
                1: (s_cond, ((cond_sb, cond), (w0_sb, w0), (b0_sb, b0[:, None]))),
                2: (s_cond2, ((w1_sb, w1), (b1_sb, b1[:, None]), (w2_sb, w2),
                              (b2_sb, b2[None, :].broadcast_to([B, NK])))),
                3: (s_cond3, ((biask[:, :], bias_k),
                              (wk_sb[:, :, 0, :], wk.rearrange("k (a g) i z -> (k a) g (i z)", g=OG)),
                              (wk_sb[:, :, 1, :], wk.rearrange("k (a g) i z -> (k a) g (i z)", g=OG))))}

            def load_x(c):
                sp.dma_start(xa[:, :, :], xt[bass.ds(c * NT, NT), :, :].rearrange("t p h -> p t h")).then_inc(s_x, 16)

            def store(c):
                for d in range(DN):
                    t, n = d // HB, d % HB
                    sp.wait_ge(s_o, DN * c + d + 1)
                    sp.dma_start(ot[c * NT + t, :, n * TOK:(n + 1) * TOK],
                                 xr[:, t, n * TOK:(n + 1) * TOK]).then_inc(s_st[t], 16)

            last_in = {}
            for e, (n, _, _, s) in enumerate(loads):
                if e in small:
                    for dst, src in small[e][1]:
                        sp.dma_start(dst, src).then_inc(small[e][0], 16)
                if e == 4:
                    load_x(0)
                if s in last_in:
                    n0, _, quant, _ = loads[last_in[s]]
                    if quant:
                        sp.wait_ge(s_q, n0 + 1)
                    else:
                        act, count = sum_count(summed.index(last_in[s]))
                        sp.wait_ge(s_sum_act if act else s_sum_dve, count)
                elif s[0] == "ys":
                    sp.wait_ge(s_yhi, KH)
                    sp.wait_ge(s_ylo, KH)
                last_in[s] = e
                sp.dma_start(raw(e), tiles[n][0]).then_inc(s_raw[s], 16)

            sp.wait_ge(s_xr, NT)
            sp.wait_ge(s_y, KH)
            load_x(1)
            store(0)
            with sp.Fori(1, NC - 1) as c:
                sp.wait_ge(s_xr, NT * c + NT)
                sp.wait_ge(s_y, KH * c + KH)
                load_x(c + 1)
                store(c)
            store(NC - 1)
            for t in range(NT):
                sp.wait_ge(s_st[t], 16 * HB * NC)

        def raw_arrived(eng, e):
            s = loads[e][3]
            eng.wait_ge(s_raw[s], 16 * sum(x[3] == s for x in loads[:e + 1]))

        @block.gpsimd
        def _(pool):
            nc.gpsimd.memset(identb[:, :], 0.0).then_inc(s_ident0, 1)
            nc.gpsimd.memset(ident, 0.0).then_inc(s_ident0, 1)
            nc.gpsimd.memset(ones[:, :], 1.0)
            nc.gpsimd.memset(onesb[:, :], 1.0)
            nc.gpsimd.memset(wsum[:, :], 0.0)
            nc.gpsimd.memset(ablk[:, :, :], 0.0)
            pool.wait_ge(s_ident0, 2)
            for m in (ident, identb[:, :]):
                nc.gpsimd.affine_select(out=m, in_=m, compare_op=ALU.not_equal, fill=1.0, base=0,
                                        pattern=[[-1, P]], channel_multiplier=1).then_inc(s_ident, 1)
            def next_chunk(c):
                nc.gpsimd.tensor_tensor(
                    bprod[:, :].rearrange("k (b o) -> k b o", o=C),
                    attT[:, bass.ds(c * BC, BC)].unsqueeze(2).broadcast_to([NK, BC, C]),
                    biask[:, :].unsqueeze(1).broadcast_to([NK, BC, C]), ALU.mult).then_inc(s_bprod, 1)
                if isinstance(c, int) and c == 0:
                    return
                for h in range(2):
                    pool.wait_ge(s_bprod if h == 0 else s_ablk, c + 1 if h == 0 else 2 * c + 1)
                    pool.sem_inc(s_turn_pool, 1)
                    block_diagonal(nc.gpsimd, c, h)

            pool.wait_ge(s_cv, 8)
            pool.wait_ge(s_cond3, 48)
            next_chunk(0)
            pool.wait_ge(s_scl, 1)
            for k in range(SCD, KH):
                nc.gpsimd.tensor_tensor(ys[:, k, :], ys[:, k, :], scl[:, :], ALU.mult).then_inc(s_yscp, 1)
            for n in range(1, NQ, 2):
                m = min(n // NG, 2)
                raw_arrived(pool, q_load[n])
                pool.wait_ge(s_thr, m + 1)
                if n >= 4:
                    pool.wait_ge(s_q, n - 3)
                elif n == 3:
                    pool.wait_ge(s_ysc, SCD)
                    pool.wait_ge(s_yscp, KH - SCD)
                rows, cols = tiles[n][1:]
                nc.gpsimd.tensor_scalar(gts[n // 2 % 2][0:rows, 0:cols], raw(q_load[n]),
                                        thr[0:rows, m:m + 1], None, ALU.is_gt).then_inc(s_gt, 1)

            def chunk(c):
                pool.wait_ge(s_y, KH * c + KH)
                pool.wait_ge(s_bb, c + 1)
                next_chunk(c + 1)

            pool.wait_ge(s_aggv, 4 * OG)
            chunk(0)
            with pool.Fori(1, NC - 1) as c:
                chunk(c)

        @block.tensor
        def _(pe):
            def mm(o, l, r, start=True, stop=True):
                return nc.tensor.matmul(o, l, r, start=start, stop=stop)

            pe.wait_ge(s_ident, 2)
            pe.wait_ge(s_cond, 48)
            nc.tensor.transpose(ps[0][:, 0:B], cond_sb, ident[0:B, 0:B]).then_inc(s_pe, 1)
            pe.wait_ge(s_cv, 1)
            mm(ps[1][:, 0:B], w0_sb, condT).then_inc(s_pe, 1)
            pe.wait_ge(s_ca, 1)
            pe.wait_ge(s_cond2, 64)
            mm(ps[2][:, 0:B], w1_sb, h1).then_inc(s_pe, 1)
            pe.wait_ge(s_ca, 2)
            mm(ps[3][0:B, 0:NK], h2, w2_sb).then_inc(s_pe, 1)
            pe.wait_ge(s_cv, 6)
            nc.tensor.transpose(ps[4][0:NK, 0:B], att, ident[0:B, 0:B]).then_inc(s_pe, 1)
            pe.wait_ge(s_cv, 7)
            nc.tensor.transpose(ps[5][:, 0:B], attr, ident[0:B, 0:B]).then_inc(s_pe, 1)
            pe.wait_ge(s_cv, 11)
            pe.wait_ge(s_cond3, 48)

            def agg_w(h, g):
                if h:
                    pe.wait_ge(s_aggv, 2 * (g + 1))
                mm(ps[g][:, :], wk_sb[:, g, :, :].rearrange("p d i -> p (d i)"),
                   attd[:, h, :, :].rearrange("p o b -> p (o b)")).then_inc(s_agg, 1)

            for g in range(OG):
                agg_w(0, g)

            def agg_b(c):
                pe.wait_ge(s_bprod, c + 1)
                if not (isinstance(c, int) and c == 0):
                    pe.wait_ge(s_p2v, c)
                mm(YB[1][:, :], ones[0:NK, :], bprod[:, :]).then_inc(s_bb, 1)

            def conv(c, k):
                if k == 0:
                    pe.wait_ge(s_x, 16 * (c + 1))
                    pe.wait_ge(s_ablk, 2 * (c + 1))
                if k == 1:
                    pe.wait_ge(s_bbv, c + 1)
                if k >= 2:
                    pe.wait_ge(s_yv, KH * c + k - 1)
                for t in range(NT):
                    last = mm(YB[k % 2][:, t * P:(t + 1) * P], xa[:, t, k * P:(k + 1) * P], ablk[:, t, :])
                last.then_inc(s_y, 1)

            def norms(c):
                pe.wait_ge(s_l1, KH * (c + 1))
                mm(YB[0][:, :], onesb[:, :], l1[:, :]).then_inc(s_norm, 1)

            def norms_T(c):
                pe.wait_ge(s_p2b, c + 1)
                for t in range(NT):
                    last = mm(YB[1][:, t:t + 1], p2b[0:1, t * P:(t + 1) * P], onesb[0:1, 0:1])
                last.then_inc(s_p2T, 1)

            def total(m):
                pe.wait_ge(s_tot, m + 1)
                pe.wait_ge(s_sum_act, sum(on_act[:(NG, 2 * NG, NQ)[m]]))
                if m == 0:
                    pe.wait_ge(s_pos, 1)
                else:
                    pe.wait_ge(s_mean, m)
                mm(YB[0][:, 0:1], ones[:, :], tot[:, m:m + 1]).then_inc(s_totm, 1)

            def transpose(n):
                rows, cols = tiles[n][1:]
                pe.wait_ge(s_q, n + 1)
                if n >= 2:
                    pe.wait_ge(s_te, n - 1)
                bank = psb[4 + n % 2]
                both = cols // (2 * P) * P
                width = both + cols % (2 * P)
                buf = msk[0:rows, n % NM, :].bitcast(bf16)
                for q in range(0, width, P):
                    w = min(P, width - q)
                    last = nc.tensor.transpose(bank[0:w, q:q + rows], buf[:, q:q + w], identb[0:rows, 0:rows])
                last.then_inc(s_t, 1)

            def waited(c):
                if not isinstance(c, int):
                    pe.sem_inc(s_turn_pe, 1)

            def group(c, j):
                if j < 4:
                    if isinstance(c, int) and c == 0:
                        pe.wait_ge(s_aggv, 2 * (OG + j + 1))
                    else:
                        pe.wait_ge(s_uv, UP * c)
                elif j - 4 < FT:
                    pe.wait_ge(s_gv, FT * c + j - 3)
                else:
                    pe.wait_ge(s_uv, UP * c + j - 3 - FT)
                waited(c)
                for k in range(KH):
                    if j == 0:
                        pe.wait_ge(s_ylo, KH * c + k + 1)
                        waited(c)
                    if j < FT:
                        w = wgT[:, k, j * P:(j + 1) * P]
                    elif j == FT:
                        w = wrT[:, k, :]
                    else:
                        w = wuT[:, k, (j - UP) * P:(j - UP + 1) * P]
                    if isinstance(c, int) and c == 0 and j == 0 and k == KH // 2:
                        transpose(1)
                    for i in range(2):
                        last = mm(GUB[j % 4][:, :], w, yp[:, k, i, :], start=(k + i == 0), stop=(k == KH - 1 and i == 1))
                last.then_inc(s_gu, 1)

            def down(c, d):
                t, n = d // HB, d % HB
                if d >= 2:
                    pe.wait_ge(s_o, DN * c + d - 1)
                elif isinstance(c, int) and c == 0:
                    pe.wait_ge(s_te, NQ)
                else:
                    pe.wait_ge(s_o, DN * c)
                cols = slice(n * TOK, (n + 1) * TOK)
                if d == 0:
                    pe.wait_ge(s_ulo, UP * c + 1)
                waited(c)
                mm(DNB[d % 2][:, :], inter_r[:, t * P:(t + 1) * P], wdT[:, FT, cols], start=True, stop=False)
                for f in range(FT):
                    if d == 0:
                        pe.wait_ge(s_ulo, UP * c + f + 2)
                        waited(c)
                    for i in range(2):
                        last = mm(DNB[d % 2][:, :], part(f, i)[:, t * P:(t + 1) * P], wdT[:, f, cols],
                                  start=False, stop=(f == FT - 1 and i == 1))
                last.then_inc(s_dn, 1)

            def downs(c, more):
                for d in range(DN):
                    down(c, d)
                    if more and d == 0:
                        norms(c + 1)
                    if more and d == 1:
                        norms_T(c + 1)

            agg_b(0)
            for k in range(KH):
                conv(0, k)
                if k % 2:
                    agg_w(1, k // 2)
            norms(0)
            norms_T(0)
            total(0)
            for what, n in order0:
                if what == "T" and n != 1:
                    transpose(n)
                elif what == "W":
                    total(n)
                elif what == "G":
                    if n == 0:
                        pe.wait_ge(s_te, 1)
                    else:
                        pe.wait_ge(s_te, n + 1)
                    group(0, n)
                elif what == "U":
                    pe.wait_ge(s_te, NG + n + 1)
                    group(0, FT + n)
                    if n == UP - 3:
                        agg_b(1)
            for k in range(KH):
                conv(1, k)
            downs(0, True)

            def chunk(c, more):
                for j in range(GU):
                    group(c, j)
                    if more and j == UP + 9:
                        agg_b(c + 1)
                    if more and j - UP - 11 in range(KH):
                        conv(c + 1, j - UP - 11)
                downs(c, more)

            with pe.Fori(1, NC - 1) as c:
                chunk(c, True)
            chunk(NC - 1, False)

        @block.scalar
        def _(act):
            def magnitudes(c, k):
                act.wait_ge(s_yv, KH * c + k + 1)
                if k >= 2:
                    act.wait_ge(s_l1, KH * c + k - 1)
                elif not (isinstance(c, int) and c == 0):
                    act.wait_ge(s_l1, KH * c)
                nc.scalar.activation(ab[:, k % 2, :], ys[:, k, :], ACT.Abs).then_inc(s_abs, 1)

            def hi_y(c, k):
                if isinstance(c, int) and c == 0 and k >= SCD:
                    act.wait_ge(s_yscp, k - SCD + 1)
                else:
                    act.wait_ge(s_ysc, KH * c + k + 1 - (0 if isinstance(c, int) and c == 0 else KH - SCD))
                nc.scalar.copy(yp[:, k, 0, :], ys[:, k, :]).then_inc(s_yhi, 1)

            def residual(c, t):
                act.wait_ge(s_x, 16 * (c + 1))
                if isinstance(c, int) and c == 0:
                    act.wait_ge(s_q, 1 + max(n for n, e in q_load.items() if loads[e][3] == ("xr", t)))
                else:
                    act.wait_ge(s_st[t], 16 * HB * c)
                nc.scalar.copy(xr[:, t, :], xa[:, t, :]).then_inc(s_xr, 1)

            def raw_sum(i):
                e = summed[i]
                n = loads[e][0]
                rows, col = tiles[n][1], hidden(n) if n < 2 * NG else n - 2 * NG
                if i == NG or i == 2 * NG:
                    act.wait_ge(s_tot, i // NG)
                raw_arrived(act, e)
                a, bufs = sum_count(i)[1], 2 if i < NG else 1
                if a > bufs:
                    act.wait_ge(s_sum_act, a - bufs)
                dst = junk[:, a % 2 * CT:(a % 2 + 1) * CT] if i < NG else g_r[:, :].bitcast(bf16)
                nc.scalar.activation(dst[0:rows, 0:tiles[n][2]], raw(e), ACT.Abs,
                                     accum_out=wsum[0:rows, col:col + 1]).then_inc(s_sum_act, 1)

            act.wait_ge(s_pe, 2)
            nc.scalar.activation(h1, ps[1][:, 0:B], ACT.Gelu, bias=b0_sb).then_inc(s_ca, 1)
            act.wait_ge(s_pe, 3)
            nc.scalar.activation(h2, ps[2][:, 0:B], ACT.Gelu, bias=b1_sb).then_inc(s_ca, 1)
            act.wait_ge(s_cv, 3)
            nc.scalar.activation(ex, lg, ACT.Exp, bias=nmx, accum_out=esum).then_inc(s_ca, 1)
            for n in (2, 3):
                raw_sum(n)

            def copy_T(n):
                act.wait_ge(s_t, n + 1)
                bank = ps8[4 + n % 2]
                pairs = bank[:, 0:KH * P].rearrange("p (q f i) -> p i q f", f=P, i=2)

                def blocks(dst):
                    return dst.rearrange("p (i q) f -> p i q f", i=2)
                if n < 2 * NG:
                    f = hidden(n)
                    if f < FT:
                        dst = (wgT, wuT)[n // NG][:, :, f * P:(f + 1) * P]
                    else:
                        dst = wrT[:, :, (n // NG) * FR:(n // NG + 1) * FR]
                    rows = tiles[n][1]
                    nc.scalar.copy(blocks(dst), pairs[:, :, :, 0:rows], saturate=False).then_inc(s_te, 1)
                    return
                r, m = divmod(n - 2 * NG, DP)
                f0, nf = m * (CT // P), min(CT // P, FT - m * (CT // P))
                last = nc.scalar.copy(blocks(wdT[:, f0:f0 + nf // 2 * 2, r * P:(r + 1) * P]),
                                      pairs[:, :, 0:nf // 2, :], saturate=False)
                if f0 + nf == FT:
                    nc.scalar.copy(wdT[:, FT - 1, r * P:(r + 1) * P], pairs[:, 0, nf // 2, :], saturate=False)
                    for h in range(2):
                        last = nc.scalar.copy(wdT[h * FR:(h + 1) * FR, FT, r * P:(r + 1) * P],
                                              pairs[0:FR, 0, nf // 2 + 1, :], saturate=False)
                last.then_inc(s_te, 1)

            for k, n in enumerate((4, 5, 6, 8, 9, 11, 12, 13)):
                raw_sum(n)
                magnitudes(0, k)
            for n, tiles_y in ((14, ()), (15, ()), (16, (0, 1)), (18, (2, 3)), (19, ()), (20, (4, 5, 6, 7))):
                raw_sum(n)
                for k in tiles_y:
                    hi_y(0, k)
            copy_T(0)

            def gate(c, f):
                act.wait_ge(s_gu, GU * c + f + 1)
                if f == 0 and not (isinstance(c, int) and c == 0):
                    act.wait_ge(s_dn, DN * c)
                if isinstance(c, int) and c == 0:
                    for n, e in q_load.items():
                        if loads[e][3] == ("inter", f // 2):
                            act.wait_ge(s_q, n + 1)
                nc.scalar.copy(inter[:, f, :], GUB[f % 4][:, :]).then_inc(s_gv, 1)

            def up(c, u):
                if u == 0:
                    act.wait_ge(s_gu, GU * c + FT + 1)
                    if isinstance(c, int) and c == 0:
                        before = [n for what, n in order0[:order0.index(("U", 0))] if what == "S"]
                        act.wait_ge(s_sum_act, sum(on_act[:max(before) + 1]))
                    nc.scalar.copy(g_r[C:P, :], GUB[FT % 4][0:C, :]).then_inc(s_gr, 1)
                    act.wait_ge(s_uv, UP * c + 1)
                    nc.scalar.copy(hi_r[C:P, :], prod[C:P, 0, :]).then_inc(s_hir, 1)
                    nc.scalar.copy(inter_r[0:C, :], prod[C:P, 0, :]).then_inc(s_uhi, 1)
                else:
                    act.wait_ge(s_uv, UP * c + u + 1)
                    nc.scalar.copy(part(u - 1, 0), prod[:, u % 2, :]).then_inc(s_uhi, 1)

            for what, n in order0:
                if what == "T" and n:
                    copy_T(n)
                elif what == "G":
                    gate(0, n)
                elif what == "U":
                    up(0, n)
                    if n - 15 in range(NT):
                        residual(0, n - 15)
                elif what == "S" and on_act[n]:
                    raw_sum(n)
            for k in range(KH):
                magnitudes(1, k)
            for k in range(KH):
                hi_y(1, k)

            def chunk(c, more):
                for f in range(FT):
                    gate(c, f)
                    if f - 4 in range(NT):
                        residual(c, f - 4)
                for u in range(UP):
                    up(c, u)
                    if more and u - 12 in range(KH):
                        magnitudes(c + 1, u - 12)
                if more:
                    for k in range(KH):
                        hi_y(c + 1, k)

            with act.Fori(1, NC - 1) as c:
                chunk(c, True)
            chunk(NC - 1, False)

        @block.vector
        def _(dve):
            V = nc.vector

            def raw_sum(i):
                e = summed[i]
                n = loads[e][0]
                rows, col = tiles[n][1], hidden(n) if n < 2 * NG else n - 2 * NG
                raw_arrived(dve, e)
                V.tensor_reduce(wsum[0:rows, col:col + 1], raw(e), AX.X, ALU.add,
                                apply_absolute_value=True).then_inc(s_sum_dve, 1)

            dve.wait_ge(s_pe, 1)
            V.tensor_copy(condT, ps[0][:, 0:B]).then_inc(s_cv, 1)
            dve.wait_ge(s_pe, 4)
            V.tensor_tensor(lg, ps[3][0:B, 0:NK], b2_sb, ALU.add).then_inc(s_cv, 1)
            dve.wait_ge(s_cv, 2)
            V.tensor_reduce(nmx, lg, AX.X, ALU.max, negate=True).then_inc(s_cv, 1)
            dve.wait_ge(s_ca, 3)
            V.reciprocal(rsum, esum).then_inc(s_cv, 1)
            dve.wait_ge(s_cv, 4)
            V.tensor_scalar(att, ex, rsum, None, ALU.mult).then_inc(s_cv, 1)
            V.tensor_reduce(mask, ident.rearrange("p (k o) -> p o k", o=OO), AX.X, ALU.add).then_inc(s_cv, 1)
            dve.wait_ge(s_cv, 5)
            V.tensor_copy(attr.rearrange("b (k o) -> b k o", o=OO),
                          att.unsqueeze(2).broadcast_to([B, NK, OO])).then_inc(s_cv, 1)
            dve.wait_ge(s_pe, 5)
            V.tensor_copy(attT[:, :], ps[4][0:NK, 0:B]).then_inc(s_cv, 1)
            dve.wait_ge(s_pe, 6)
            V.tensor_copy(attrT, ps[5][:, 0:B]).then_inc(s_cv, 1)
            dve.wait_ge(s_cv, 9)
            for h in range(2):
                V.tensor_tensor(attd[:, h, :, :],
                                attrT[:, h * B // 2:(h + 1) * B // 2].unsqueeze(1).broadcast_to([P, OO, B // 2]),
                                mask.unsqueeze(2).broadcast_to([P, OO, B // 2]), ALU.mult).then_inc(s_cv, 1)
            for g in range(OG):
                dve.wait_ge(s_agg, g + 1)
                agg_copy(0, g)
                if g < 2:
                    raw_sum(g)
            dve.wait_ge(s_aggv, 2 * OG)
            for h in range(2):
                block_diagonal(V, 0, h)

            def agg_b(c):
                dve.wait_ge(s_bb, c + 1)
                V.tensor_copy(bbc[:, :], YB[1][:, :]).then_inc(s_bbv, 1)

            def conv(c, k):
                dve.wait_ge(s_y, KH * c + k + 1)
                if k == 0:
                    dve.wait_ge(s_bbv, c + 1)
                    if not (isinstance(c, int) and c == 0):
                        dve.wait_ge(s_yhi, KH * c)
                        dve.wait_ge(s_ylo, KH * c)
                V.tensor_tensor(ys[:, k, :], YB[k % 2][:, :], bbc[:, :], ALU.add).then_inc(s_yv, 1)
                if k >= 1:
                    add_l1(c, k - 1)
                if k == KH - 1:
                    add_l1(c, k)

            def add_l1(c, k):
                dve.wait_ge(s_abs, KH * c + k + 1)
                if k == 0:
                    if not (isinstance(c, int) and c == 0):
                        dve.wait_ge(s_norm, c)
                    V.tensor_copy(l1[:, :], ab[:, 0, :]).then_inc(s_l1, 1)
                else:
                    dve.wait_ge(s_l1, KH * c + k)
                    V.tensor_tensor(l1[:, :], l1[:, :], ab[:, k % 2, :], ALU.add).then_inc(s_l1, 1)

            def scales(c):
                dve.wait_ge(s_norm, c + 1)
                V.tensor_scalar(p2[:, :], YB[0][:, :], 2.0 ** -60, None, ALU.max).then_inc(s_pos, 1)
                dve.wait_ge(s_pos, c + 1)
                V.tensor_scalar(p2[:, :].bitcast(i32), p2[:, :].bitcast(i32), EXPONENT, None,
                                ALU.bitwise_and).then_inc(s_p2, 1)
                dve.wait_ge(s_p2, c + 1)
                V.tensor_scalar(scl[:, :].bitcast(i32), p2[:, :].bitcast(i32), -1.0,
                                float((2 * 127 + L1_LOG) << 23), ALU.mult, ALU.add).then_inc(s_scl, 1)
                V.tensor_copy(p2b[:, :], p2[0:1, :]).then_inc(s_p2b, 1)
                dve.wait_ge(s_scl, c + 1)

            def scale_y(c, k):
                V.tensor_tensor(ys[:, k, :], ys[:, k, :], scl[:, :], ALU.mult).then_inc(s_ysc, 1)

            def split_y(c, k):
                dve.wait_ge(s_yhi, KH * c + k + 1)
                V.tensor_tensor(yp[:, k, 1, :], ys[:, k, :], yp[:, k, 0, :], ALU.subtract).then_inc(s_ylo, 1)

            def out_scales(c):
                dve.wait_ge(s_p2T, c + 1)
                V.tensor_copy(p2t[:, :], YB[1][:, 0:NT]).then_inc(s_p2v, 1)

            def out_scales2(c):
                dve.wait_ge(s_p2v, c + 1)
                dve.wait_ge(s_kk, 3)
                V.scalar_tensor_tensor(osc[:, :], p2t[:, :], kk[:, 2:3], p2t[:, :],
                                       ALU.mult, ALU.mult).then_inc(s_osc, 1)

            def partition_sums(m, n):
                i = (NG, 2 * NG, NQ)[m]
                dve.wait_ge(s_sum_act, sum(on_act[:i]))
                dve.wait_ge(s_sum_dve, i - sum(on_act[:i]))
                V.tensor_reduce(tot[:, m:m + 1], wsum[:, 0:n], AX.X, ALU.add).then_inc(s_tot, 1)

            def threshold(m):
                dve.wait_ge(s_totm, m + 1)
                V.tensor_scalar(mean[:, m:m + 1], YB[0][:, 0:1], 1.0 / (F * H), None, ALU.mult).then_inc(s_mean, 1)
                dve.wait_ge(s_mean, m + 1)
                V.tensor_scalar(nthr[:, m:m + 1], mean[:, m:m + 1], EPS, -0.5, ALU.add, ALU.mult)
                V.tensor_scalar(thr[:, m:m + 1], mean[:, m:m + 1], EPS, 0.5, ALU.add, ALU.mult).then_inc(s_thr, 1)
                dve.wait_ge(s_thr, m + 1)

            def quantise(n):
                m, e = min(n // NG, 2), q_load[n]
                rows = tiles[n][1]
                if n % 2 == 0:
                    raw_arrived(dve, e)
                    if n >= NM:
                        dve.wait_ge(s_t, n - NM + 1)
                    for src, gt, _ in quantised(n):
                        last = V.tensor_scalar(gt, src, thr[0:rows, m:m + 1], None, ALU.is_gt, saturate=False)
                    last.then_inc(s_gtv, 1)
                    dve.wait_ge(s_gtv, n // 2 + 1)
                else:
                    dve.wait_ge(s_gt, (n + 1) // 2)
                    if n >= NM:
                        dve.wait_ge(s_t, n - NM + 1)
                for src, gt, dst in quantised(n):
                    last = V.scalar_tensor_tensor(dst, src, nthr[0:rows, m:m + 1], gt, ALU.is_lt, ALU.subtract,
                                                  saturate=False)
                last.then_inc(s_q, 1)

            def weight_scales():
                V.tensor_scalar(kk[:, 0:1], mean[:, 0:1], -(2.0 ** -(2 * L1_LOG)) / PROD, None, ALU.mult).then_inc(s_kk, 1)
                dve.wait_ge(s_kk, 1)
                V.tensor_tensor(kk[:, 1:2], kk[:, 0:1], mean[:, 1:2], ALU.mult).then_inc(s_kk, 1)
                dve.wait_ge(s_kk, 2)
                V.tensor_tensor(kk[:, 2:3], kk[:, 1:2], mean[:, 2:3], ALU.mult).then_inc(s_kk, 1)

            def product(c, u):
                dve.wait_ge(s_gu, GU * c + FT + u + 1)
                if u >= 2:
                    dve.wait_ge(s_uhi, UP * c + u - 1)
                    dve.wait_ge(s_ulo, UP * c + u - 1)
                elif not (isinstance(c, int) and c == 0):
                    dve.wait_ge(s_uhi, UP * c)
                    dve.wait_ge(s_ulo, UP * c)
                bank = GUB[(FT + u) % 4]
                if u == 0:
                    dve.wait_ge(s_gr, c + 1)
                    V.scalar_tensor_tensor(prod[C:P, 0, :], bank[C:P, :], PROD, g_r[C:P, :],
                                           ALU.mult, ALU.mult).then_inc(s_uv, 1)
                else:
                    dve.wait_ge(s_gv, FT * c + u)
                    V.scalar_tensor_tensor(prod[:, u % 2, :], bank[:, :], PROD, inter[:, u - 1, :],
                                           ALU.mult, ALU.mult).then_inc(s_uv, 1)

            def split(c, u):
                if u == 0:
                    dve.wait_ge(s_hir, c + 1)
                    dve.wait_ge(s_uhi, UP * c + 1)
                    if not (isinstance(c, int) and c == 0):
                        dve.wait_ge(s_dn, DN * c)
                    V.tensor_tensor(inter_r[C:P, :], prod[C:P, 0, :], hi_r[C:P, :], ALU.subtract).then_inc(s_ulo, 1)
                else:
                    dve.wait_ge(s_uhi, UP * c + u + 1)
                    V.tensor_tensor(part(u - 1, 1), prod[:, u % 2, :], part(u - 1, 0),
                                    ALU.subtract).then_inc(s_ulo, 1)

            def output(c, d):
                t, n = d // HB, d % HB
                dve.wait_ge(s_dn, DN * c + d + 1)
                if n == 0:
                    dve.wait_ge(s_xr, NT * c + t + 1)
                cols = slice(n * TOK, (n + 1) * TOK)
                V.scalar_tensor_tensor(xr[:, t, cols], DNB[d % 2][:, :], osc[:, t:t + 1], xr[:, t, cols],
                                       ALU.mult, ALU.add).then_inc(s_o, 1)

            agg_b(0)
            for k in range(KH):
                conv(0, k)
                if k in (2, 4, 6, 7):
                    g = (k - 1) // 2
                    dve.wait_ge(s_agg, OG + g + 1)
                    agg_copy(1, g)
                if k in (3, 5):
                    raw_sum(7 if k == 3 else 10)
            scales(0)
            for k in range(SCD):
                scale_y(0, k)
            raw_sum(17)
            for k in range(4):
                split_y(0, k)
            raw_sum(21)
            partition_sums(0, NG)
            split_y(0, 4)
            threshold(0)
            quantise(0)
            for k in range(5, KH):
                split_y(0, k)
            out_scales(0)
            for n in range(1, NM):
                quantise(n)
            ends = (NG, 2 * NG, NQ)
            for what, n in order0:
                if what == "T" and n + NM not in range(ends[min(n // NG, 2)], ends[min(n // NG, 2)] + NM):
                    quantise(n + NM)
                if what == "S" and not on_act[n]:
                    raw_sum(n)
                if what == "M":
                    partition_sums(n, (NG, ND)[n - 1])
                if what == "W":
                    threshold(n)
                    quantise(n * NG)
                if what == "Q":
                    quantise(n)
                if what == "U":
                    if n == UP - 2:
                        agg_b(1)
                    product(0, n)
                    if n >= 1:
                        split(0, n - 1)
                    if n == UP // 2:
                        weight_scales()
                        out_scales2(0)
            conv(1, 0)
            split(0, UP - 1)
            for k in range(1, KH):
                conv(1, k)

            def outputs(c, more):
                output(c, 0)
                if more:
                    scales(c + 1)
                    for k in range(KH):
                        scale_y(c + 1, k)
                for d in range(1, DN):
                    output(c, d)
                    if more:
                        split_y(c + 1, d - 1)
                if more:
                    split_y(c + 1, KH - 1)
                    out_scales(c + 1)
                    out_scales2(c + 1)

            outputs(0, True)

            def chunk(c, more):
                for u in range(UP):
                    product(c, u)
                    if u >= 1:
                        split(c, u - 1)
                    if more and u == 11:
                        agg_b(c + 1)
                    if more and u - 12 in range(KH):
                        conv(c + 1, u - 12)
                split(c, UP - 1)
                outputs(c, more)

            with dve.Fori(1, NC - 1) as c:
                chunk(c, True)
            chunk(NC - 1, False)


_INS = ['x', 'cond_128', 'L0_cond_W0', 'L0_cond_b0', 'L0_cond_W1', 'L0_cond_b1', 'L0_cond_W2', 'L0_cond_b2',
        'L0_cond_weight', 'L0_cond_bias_k', 'L0_ffn_w_gate', 'L0_ffn_w_up', 'L0_ffn_w_down']
_OUTS = [((64, 64, 1024), 'float32')]


def kernel(**inputs):
    import numpy as _np
    import concourse.bacc as _bacc
    from concourse import mybir as _mybir
    from concourse.bass_utils import run_bass_kernel_spmd as _run

    nc = _bacc.Bacc("TRN2", target_bir_lowering=False, num_devices=1)
    arrays, args = {}, []
    for name in _INS:
        a = _np.ascontiguousarray(inputs[name])
        arrays[f"in_{name}_dram"] = a
        args.append(nc.dram_tensor(f"in_{name}_dram", a.shape, _mybir.dt.from_np(a.dtype), kind="ExternalInput").ap())
    for i, (shape, dtype) in enumerate(_OUTS):
        dt = _mybir.dt.from_np(_np.dtype(dtype))
        args.append(nc.dram_tensor(f"out_{i}_dram", shape, dt, kind="ExternalOutput").ap())
    adaln_ternary_ffn(nc, *args)
    r = _run(nc, [arrays], core_ids=[0])
    return r.results[0]["out_0_dram"]
```
